# Optimizing a Trainium2 kernel written in Bass

```python
import numpy as np
import jax
import jax.numpy as jnp

def _softmax(x, axis=-1):
    return jax.nn.softmax(x, axis=axis)

def _gelu(x):
    return jax.nn.gelu(x, approximate=True)

def _silu(x):
    return jax.nn.silu(x)

def _sigmoid(x):
    return jax.nn.sigmoid(x)

def _layernorm(x, axis=-1, eps=1e-05):
    m = jnp.mean(x, axis=axis, keepdims=True)
    v = jnp.var(x, axis=axis, keepdims=True)
    return (x - m) / jnp.sqrt(v + eps)

def _scatter_add(tgt, idx, src, axis=0):
    return tgt.at[idx].add(src)

def _segment_sum(src, seg, n):
    return jax.ops.segment_sum(src, seg, n)
kernel_name = 'mk_gps_d1_gnn_r8_da7639'

def setup_inputs(seed: int=0):
    np.random.seed(seed)
    _w = jnp.asarray

    def _rec_inputs():
        import jax
        import jax.numpy as jnp
        _gk = jax.random.key(seed)
        x = -0.0002117 + 1 * jax.random.normal(jax.random.fold_in(_gk, 1), (6250, 256), jnp.float32)
        _s = jax.random.randint(jax.random.fold_in(_gk, 2), (50000,), 0, 6250, jnp.int32)
        _d = jax.random.randint(jax.random.fold_in(_gk, 3), (50000,), 0, 6250, jnp.int32)
        _loop = jnp.arange(6250, dtype=jnp.int32)
        src = jnp.concatenate([_s, _d, _loop])
        dst = jnp.concatenate([_d, _s, _loop])
        _o = jnp.argsort(dst, stable=True)
        src = src[_o]
        dst = dst[_o]
        edge_attr_256 = -5.16925e-05 + 1.00005 * jax.random.normal(jax.random.fold_in(_gk, 12), (106250, 256), jnp.float32)
        return (x, src, dst, edge_attr_256)
    x, src, dst, edge_attr_256 = _rec_inputs()

    def _L0_gnn_setup():
        import jax, jax.numpy as jnp
        import numpy as np
        N_NODES = 12500
        N_EDGES = 50000
        C = 256
        NUM_GRAPHS = 512
        EPS = 1e-05
        key = jax.random.key(seed)
        ks = jax.random.split(key, 12)
        x = jax.random.normal(ks[0], (N_NODES, C), dtype=jnp.float32)
        edge_index = jax.random.randint(ks[1], (2, N_EDGES), 0, N_NODES, dtype=jnp.int32)
        edge_attr = jax.random.normal(ks[2], (N_EDGES, C), dtype=jnp.float32)
        batch = jnp.sort(jax.random.randint(ks[3], (N_NODES,), 0, NUM_GRAPHS, dtype=jnp.int32))
        s1 = 1.0 / np.sqrt(C)
        s2 = 1.0 / np.sqrt(2 * C)
        W1 = jax.random.normal(ks[4], (C, 2 * C), dtype=jnp.float32) * s1
        b1 = jnp.zeros((2 * C,), dtype=jnp.float32)
        bn_gamma = jnp.ones((2 * C,), dtype=jnp.float32)
        bn_beta = jnp.zeros((2 * C,), dtype=jnp.float32)
        W2 = jax.random.normal(ks[5], (2 * C, C), dtype=jnp.float32) * s2
        b2 = jnp.zeros((C,), dtype=jnp.float32)
        ln_w = jnp.ones((C,), dtype=jnp.float32)
        ln_b = jnp.zeros((C,), dtype=jnp.float32)
        gn_w = jnp.ones((C,), dtype=jnp.float32)
        gn_b = jnp.zeros((C,), dtype=jnp.float32)
        gn_ms = jnp.ones((C,), dtype=jnp.float32)
        return dict(x=x, edge_index=edge_index, edge_attr=edge_attr, batch=batch, W1=W1, b1=b1, bn_gamma=bn_gamma, bn_beta=bn_beta, W2=W2, b2=b2, ln_w=ln_w, ln_b=ln_b, gn_w=gn_w, gn_b=gn_b, gn_ms=gn_ms)
    _L0_gnn_all = _L0_gnn_setup()
    _L0_gnn_in = {k: v for k, v in _L0_gnn_all.items() if k in ('W1', 'b1', 'bn_gamma', 'bn_beta', 'W2', 'b2', 'ln_w', 'ln_b', 'gn_w', 'gn_b', 'gn_ms')}
    del _L0_gnn_all

    def _L0_mix_setup():
        import math
        import jax, jax.numpy as jnp
        import numpy as np
        EPS_DIV = 1e-07
        EPS_NORM = 1e-12

        def _l2_normalize(x, axis):
            n = jnp.sqrt(jnp.sum(x * x, axis=axis, keepdims=True))
            return x / jnp.maximum(n, EPS_NORM)
        key = jax.random.key(seed)
        ks = jax.random.split(key, 5)
        b, N, C = (8, 512, 256)
        x = jax.random.normal(ks[0], (b, N, C), dtype=jnp.float32)
        W_qkv = jax.random.normal(ks[1], (C, 3 * C), dtype=jnp.float32) * (1.0 / math.sqrt(C))
        b_qkv = jax.random.normal(ks[2], (3 * C,), dtype=jnp.float32) * 0.02
        W_out = jax.random.normal(ks[3], (C, C), dtype=jnp.float32) * (1.0 / math.sqrt(C))
        b_out = jax.random.normal(ks[4], (C,), dtype=jnp.float32) * 0.02
        return {'x': x, 'W_qkv': W_qkv, 'b_qkv': b_qkv, 'W_out': W_out, 'b_out': b_out}
    _L0_mix_all = _L0_mix_setup()
    _L0_mix_in = {k: v for k, v in _L0_mix_all.items() if k in ('W_qkv', 'b_qkv', 'W_out', 'b_out')}
    del _L0_mix_all

    def _L0_ffn_setup():
        import jax, jax.numpy as jnp
        import numpy as np
        N_EXPERTS = 8
        TOP_K = 2
        key = jax.random.key(seed)
        ks = jax.random.split(key, 5)
        B, T, C, E, H = (8, 256, 256, 8, 682)
        scale = 1.0 / np.sqrt(C)
        return {'x': jax.random.normal(ks[0], (B, T, C), dtype=jnp.float32), 'router_w': jax.random.normal(ks[1], (E, C), dtype=jnp.float32) * scale, 'w1': jax.random.normal(ks[2], (E, H, C), dtype=jnp.float32) * scale, 'w2': jax.random.normal(ks[3], (E, C, H), dtype=jnp.float32) * (1.0 / np.sqrt(H)), 'w3': jax.random.normal(ks[4], (E, H, C), dtype=jnp.float32) * scale}
    _L0_ffn_all = _L0_ffn_setup()
    _L0_ffn_in = {k: v for k, v in _L0_ffn_all.items() if k in ('router_w', 'w1', 'w2', 'w3')}
    del _L0_ffn_all
    return {'x': x, 'src': src, 'dst': dst, 'edge_attr_256': edge_attr_256, 'L0_gnn_W1': _L0_gnn_in['W1'], 'L0_gnn_b1': _L0_gnn_in['b1'], 'L0_gnn_bn_gamma': _L0_gnn_in['bn_gamma'], 'L0_gnn_bn_beta': _L0_gnn_in['bn_beta'], 'L0_gnn_W2': _L0_gnn_in['W2'], 'L0_gnn_b2': _L0_gnn_in['b2'], 'L0_gnn_ln_w': _L0_gnn_in['ln_w'], 'L0_gnn_ln_b': _L0_gnn_in['ln_b'], 'L0_gnn_gn_w': _L0_gnn_in['gn_w'], 'L0_gnn_gn_b': _L0_gnn_in['gn_b'], 'L0_gnn_gn_ms': _L0_gnn_in['gn_ms'], 'L0_mix_W_qkv': _L0_mix_in['W_qkv'], 'L0_mix_b_qkv': _L0_mix_in['b_qkv'], 'L0_mix_W_out': _L0_mix_in['W_out'], 'L0_mix_b_out': _L0_mix_in['b_out'], 'L0_ffn_router_w': _L0_ffn_in['router_w'], 'L0_ffn_w1': _L0_ffn_in['w1'], 'L0_ffn_w2': _L0_ffn_in['w2'], 'L0_ffn_w3': _L0_ffn_in['w3']}

def reference(x, src, dst, edge_attr_256, L0_gnn_W1, L0_gnn_b1, L0_gnn_bn_gamma, L0_gnn_bn_beta, L0_gnn_W2, L0_gnn_b2, L0_gnn_ln_w, L0_gnn_ln_b, L0_gnn_gn_w, L0_gnn_gn_b, L0_gnn_gn_ms, L0_mix_W_qkv, L0_mix_b_qkv, L0_mix_W_out, L0_mix_b_out, L0_ffn_router_w, L0_ffn_w1, L0_ffn_w2, L0_ffn_w3):
    import jax
    import jax.numpy as jnp

    def _L0_gnn_ref(x, edge_index, edge_attr, batch, W1, b1, bn_gamma, bn_beta, W2, b2, ln_w, ln_b, gn_w, gn_b, gn_ms):
        import jax, jax.numpy as jnp
        import numpy as np
        N_NODES = 12500
        N_EDGES = 50000
        C = 256
        NUM_GRAPHS = 512
        EPS = 1e-05
        src, dst = (edge_index[0], edge_index[1])
        msg = jax.nn.relu(x[src] + edge_attr)
        agg = jnp.zeros_like(x).at[dst].add(msg)
        h = x + agg
        h = h @ W1 + b1
        mu = jnp.mean(h, axis=0)
        var = jnp.mean((h - mu) ** 2, axis=0)
        h = (h - mu) / jnp.sqrt(var + EPS) * bn_gamma + bn_beta
        h = jax.nn.relu(h) @ W2 + b2
        cnt = jax.ops.segment_sum(jnp.ones((h.shape[0],), h.dtype), batch, NUM_GRAPHS)
        denom = jnp.maximum(cnt, 1.0) * C
        mean_g = jax.ops.segment_sum(h.sum(axis=1), batch, NUM_GRAPHS) / denom
        h = h - mean_g[batch][:, None]
        var_g = jax.ops.segment_sum((h * h).sum(axis=1), batch, NUM_GRAPHS) / denom
        h = h * jax.lax.rsqrt(var_g + EPS)[batch][:, None] * ln_w + ln_b
        cnt_c = jnp.maximum(cnt, 1.0)[:, None]
        mean = jax.ops.segment_sum(h, batch, NUM_GRAPHS) / cnt_c
        out = h - mean[batch] * gn_ms
        var2 = jax.ops.segment_sum(out * out, batch, NUM_GRAPHS) / cnt_c
        out = out * jax.lax.rsqrt(var2 + EPS)[batch] * gn_w + gn_b
        out = jax.nn.relu(out)
        return x + out

    def _L0_mix_ref(x, W_qkv, b_qkv, W_out, b_out):
        import math
        import jax, jax.numpy as jnp
        import numpy as np
        EPS_DIV = 1e-07
        EPS_NORM = 1e-12

        def _l2_normalize(x, axis):
            n = jnp.sqrt(jnp.sum(x * x, axis=axis, keepdims=True))
            return x / jnp.maximum(n, EPS_NORM)
        b, N, C = x.shape
        qkv = x @ W_qkv + b_qkv
        q, k, v = jnp.split(qkv, 3, axis=2)
        q = q - jnp.mean(q, axis=2, keepdims=True)
        k = k - jnp.mean(k, axis=2, keepdims=True)
        q2 = q * q
        k2 = k * k
        q2s = jnp.sum(q2, axis=2, keepdims=True)
        k2s = jnp.sum(k2, axis=2, keepdims=True)
        k2 = _l2_normalize(k2 / (k2s + EPS_DIV), axis=-2)
        q2 = _l2_normalize(q2 / (q2s + EPS_DIV), axis=-1)
        kv = jnp.einsum('bnc,bnd->bcd', k2, v)
        t2 = jnp.einsum('bnc,bcd->bnd', q2, kv) / math.sqrt(N)
        attn = v + t2
        return attn @ W_out + b_out

    def _L0_ffn_ref(x, router_w, w1, w2, w3):
        import jax, jax.numpy as jnp
        import numpy as np
        N_EXPERTS = 8
        TOP_K = 2
        B, T, C = x.shape
        flat = x.reshape(-1, C)
        logits = flat @ router_w.T
        probs = jax.nn.softmax(logits, axis=-1)
        topk_probs, topk_idx = jax.lax.top_k(probs, TOP_K)
        topk_probs = topk_probs / (jnp.sum(topk_probs, axis=-1, keepdims=True) + 1e-09)
        onehot = jax.nn.one_hot(topk_idx, N_EXPERTS, dtype=flat.dtype)
        gates = jnp.einsum('nk,nke->ne', topk_probs, onehot)
        h1 = jnp.einsum('nc,ehc->neh', flat, w1)
        h3 = jnp.einsum('nc,ehc->neh', flat, w3)
        h = jax.nn.silu(h1) * h3
        y = jnp.einsum('neh,ech->nec', h, w2)
        out = jnp.einsum('ne,nec->nc', gates, y)
        return out.reshape(B, T, C)
    edge_index = jnp.stack([src, dst])
    batch0 = jnp.zeros((6250,), jnp.int32)
    xn = _layernorm(x, axis=-1)
    x = x + _L0_gnn_ref(xn, edge_index, edge_attr_256, batch0, L0_gnn_W1, L0_gnn_b1, L0_gnn_bn_gamma, L0_gnn_bn_beta, L0_gnn_W2, L0_gnn_b2, L0_gnn_ln_w, L0_gnn_ln_b, L0_gnn_gn_w, L0_gnn_gn_b, L0_gnn_gn_ms) + _L0_mix_ref(xn[None], L0_mix_W_qkv, L0_mix_b_qkv, L0_mix_W_out, L0_mix_b_out)[0]
    x = x + _L0_ffn_ref(_layernorm(x, axis=-1)[None], L0_ffn_router_w, L0_ffn_w1, L0_ffn_w2, L0_ffn_w3)[0]
    return x

_drawn_inputs = setup_inputs


def setup_inputs(seed=0):
    import zlib

    import numpy as np

    out = dict(_drawn_inputs(seed))
    spreads = {'L0_gnn_b1': (0.0, 0.8),
     'L0_gnn_bn_gamma': (1.0, 0.2),
     'L0_gnn_bn_beta': (0.0, 0.1),
     'L0_gnn_b2': (0.0, 0.458),
     'L0_gnn_ln_w': (1.0, 0.6),
     'L0_gnn_ln_b': (0.0, 0.545),
     'L0_gnn_gn_w': (1.0, 0.2),
     'L0_gnn_gn_b': (0.0, 0.1),
     'L0_gnn_gn_ms': (1.0, 0.2)}
    factors = {'L0_mix_b_out': 3.891}
    for name, (base, spread) in spreads.items():
        noise = np.random.default_rng([zlib.crc32(name.encode()), seed]).standard_normal(out[name].shape)
        drawn = base * np.exp(spread * noise) if base else spread * noise
        out[name] = jnp.asarray(drawn.astype(out[name].dtype))
    for name, factor in factors.items():
        out[name] = (out[name] * factor).astype(out[name].dtype)
    return out
```

```python
import math
from contextlib import ExitStack

import concourse.bass as bass
from concourse import mybir

F32 = mybir.dt.float32
F16 = mybir.dt.float16
I32 = mybir.dt.int32
ALU = mybir.AluOpType
ACT = mybir.ActivationFunctionType
AX = mybir.AxisListType

N = 6250
C = 256
E = 106250
CB = C // 128
TR = 125
NT = N // TR
HID = 2 * C
FB = HID // 128
CH = 250
NC = N // CH
EB = 1024
EK = EB // 128
NB = -(-E // EB)
LAST = E - EB
SEEN = (NB - 1) * EB - LAST
WIN = 128
NX = 8
H = 682
HB = -(-H // 128)
TAIL = H - 128 * (HB - 1)
PAIRS = 2 * N
WL = 2 * CB * H + HB * C
FT = -(-PAIRS // 128) + NX
ROW = C + 4
EPS = 1e-5
EPS_DIV = 1e-7
EPS_NORM = 1e-12
SX, SW, SG = 64.0, 256.0, 16.0


class K:
    pass


def pairs(eng, n, body):
    for h in range(2):
        body(h, h)
    with eng.Fori(1, n // 2) as i:
        for h in range(2):
            body(i * 2 + h, h)
    if n % 2:
        body(n - 1, (n - 1) % 2)


def first_two(n):
    return isinstance(n, int) and n < 2


def build(nc, A, out):
    k = K()
    with ExitStack() as ctx:
        k.nc, k.A, k.out = nc, A, out
        k.sem = lambda name: ctx.enter_context(nc.semaphore(name))
        k.psum = [ctx.enter_context(nc.psum_tensor(f"bank{i}", [128, 512], F32)) for i in range(8)]

        def sb(name, shape, dt=F32, where=ctx):
            return where.enter_context(nc.sbuf_tensor(name, shape, dt))

        k.sb = sb
        k.xn_d = nc.dram_tensor("xn_rows", (N, C), F32, kind="Internal").ap()
        k.tok_d = nc.dram_tensor("token_rows", (N, ROW), F32, kind="Internal").ap()
        k.r_d = nc.dram_tensor("residual_rows", (N, C), F32, kind="Internal").ap()
        k.acc_d = nc.dram_tensor("output_rows", (N + 128, C), F32, kind="Internal").ap()
        k.disp_d = nc.dram_tensor("dispatched_rows", ((FT + 1) * 128, ROW), F32, kind="Internal").ap()
        k.ident = sb("ident", [128, 128])
        k.ones = sb("ones", [128, 128])
        k.rwT = sb("router_wT", [128, CB, NX])
        k.hmask = sb("hidden_mask", [128, 1])
        k.consts = k.sem("consts_ready")
        k.eps = sb("eps", [128, 1])
        k.pool_turn = k.sem("pool_turn")
        k.CONST = 6
        k.LG = sb("logits", [TR, NT, NX])
        k.gsc = sb("norm_scale", [128, CB])
        k.gbi = sb("norm_bias", [128, CB])
        with ExitStack() as big:
            k.UT = sb("node_sumT", [128, CB, N + WIN], F32, big)
            with ExitStack() as mid:
                k.XNT = sb("xnT", [128, CB, N], F32, mid)
                with ExitStack() as low:
                    tables(k, low)
                    with ExitStack() as st:
                        layernorm_stage(k, st)
                    with ExitStack() as st:
                        edge_mix_stage(k, st)
            with ExitStack() as st:
                gnn_mlp_stage(k, st)
            with ExitStack() as st:
                residual_stage(k, st)
        with ExitStack() as st:
            moe_stage(k, st)


def tables(k, st):
    k.src = k.sb("src_table", [128, NB + 2, EK], I32, st)
    k.dstl = k.sb("dst_in_window", [128, NB, EK], F32, st)
    k.basei = k.sb("window_base", [1, NB], I32, st)
    k.wqkv = k.sb("w_qkv", [128, CB, 3 * C], F32, st)
    k.wout = k.sb("w_out", [128, CB, C], F32, st)
    k.bq = k.sb("b_q", [128, CB], F32, st)
    k.bkv = k.sb("b_kv_rows", [128, 2 * C], F32, st)
    k.vwi = k.sb("w_v_out_plus_identity", [128, CB, C], F32, st)
    k.bb = k.sb("bias_rows", [128, C], F32, st)
    k.iota = k.sb("iota_window", [128, WIN], F32, st)


def layernorm_stage(k, st):
    nc, sb, sem, A = k.nc, k.sb, k.sem, k.A
    G = 5
    NG = NT // G
    X = [sb(f"x_in{h}", [TR, G, C], F32, st) for h in range(2)]
    XN = [sb(f"xn{h}", [TR, G, C], F32, st) for h in range(2)]
    stats = sb("ln_stats", [TR, G, 6], F32, st)
    mv = sb("ln_mv", [TR, G, 2], F32, st)
    rstd = sb("ln_rstd", [TR, G], F32, st)
    std = sb("ln_std", [TR, G], F32, st)
    var_done, std_done = sem("ln_var_done"), sem("ln_std_done")
    dsti = sb("dst_table", [128, NB, EK], I32, st)
    basef = sb("window_base_f", [1, NB], F32, st)
    bq_row = sb("b_qkv_rows", [128, 3 * C], F32, st)
    b_out_row = sb("b_out_rows", [128, C], F32, st)
    bv_col = sb("b_v", [128, CB], F32, st)
    bv_wide = sb("b_v_wide", [128, CB, 128], F32, st)
    wvT = sb("w_vT", [128, CB, C], F32, st)
    msum = sb("mean_sums", [128, 2, CB + 1], F32, st)
    rw = sb("router_w", [NX, C], F32, st)
    x_in = [sem(f"x_in_{h}") for h in range(2)]
    xn_done, x_free, xn_st = sem("xn_done"), sem("x_free"), [sem(f"xn_stored_{h}") for h in range(2)]
    tr_full, tr_free = sem("tr_full"), sem("tr_free")
    tab_in, seen_out, prep_v, prep_p, base_full = sem("tables_in"), sem("seen_masked"), sem("prep_vector"), sem("prep_tensor"), sem("base_full")
    tail0 = sem("tail_zeroed")
    k.seen_out = seen_out
    TAB = 16 * 13
    bank = k.psum

    with nc.Block() as block:
        @block.sync
        def _(sp):
            def load(n, h):
                sp.wait_ge(x_free, n + 1)
                sp.dma_start(X[h][:, :, :], A["x"][bass.ds(n * (G * TR), G * TR), :]
                             .rearrange("(g p) c -> p g c", g=G)).then_inc(x_in[h], 16)

            pairs(sp, NG, load)

        @block.scalar
        def _(act):
            body = (NB - 1) * EB
            t = lambda name: A[name]
            act.dma_start(dsti[:, 0:NB - 1, :], t("dst")[0:body].rearrange("(b p k) -> p b k", p=128, k=EK)).then_inc(tab_in, 16)
            act.dma_start(dsti[:, NB - 1, :], t("dst")[LAST:E].rearrange("(p k) -> p k", k=EK)).then_inc(tab_in, 16)
            act.dma_start(k.src[:, 0:NB - 1, :], t("src")[0:body].rearrange("(b p k) -> p b k", p=128, k=EK)).then_inc(tab_in, 16)
            act.dma_start(k.src[:, NB - 1, :], t("src")[LAST:E].rearrange("(p k) -> p k", k=EK)).then_inc(tab_in, 16)
            with nc.allow_non_contiguous_dma("one word of each batch"):
                act.dma_start(k.basei[0:1, 0:NB - 1], t("dst")[0:body].rearrange("(a b k) -> a b k", a=1, k=EB)[:, :, 0]).then_inc(tab_in, 16)
                act.dma_start(k.basei[0:1, NB - 1:NB], t("dst")[LAST:LAST + 1].rearrange("(a b) -> a b", a=1)).then_inc(tab_in, 16)
                act.dma_start(k.bq[:, :], t("L0_mix_b_qkv")[0:C].rearrange("(b p) -> p b", p=128)).then_inc(tab_in, 16)
                act.dma_start(bv_col[:, :], t("L0_mix_b_qkv")[2 * C:3 * C].rearrange("(b p) -> p b", p=128)).then_inc(tab_in, 16)
            act.dma_start(k.wqkv[:, :, :], t("L0_mix_W_qkv").rearrange("(b p) n -> p b n", p=128)).then_inc(tab_in, 16)
            act.dma_start(k.wout[:, :, :], t("L0_mix_W_out").rearrange("(b p) n -> p b n", p=128)).then_inc(tab_in, 16)
            act.dma_start(bq_row[:, :], t("L0_mix_b_qkv").partition_broadcast(128)).then_inc(tab_in, 16)
            act.dma_start(b_out_row[:, :], t("L0_mix_b_out").partition_broadcast(128)).then_inc(tab_in, 16)
            act.dma_start(rw[:, :], t("L0_ffn_router_w")).then_inc(tab_in, 16)

            def copy_out(n, h):
                act.wait_ge(k.consts, k.CONST)
                act.wait_ge(var_done, n + 1)
                act.activation(std[:, :], mv[:, :, 1], ACT.Sqrt, bias=k.eps[0:TR, :]).then_inc(std_done, 1)
                for g in range(G):
                    m = n * G + g
                    act.wait_ge(k.consts, k.CONST)
                    act.wait_ge(tr_full, m + 1)
                    p = bank[g][:, 0:CB * TR].rearrange("p (b c) -> p b c", b=CB)
                    act.activation(k.XNT[:, :, bass.ds(m * TR, TR)], p, ACT.Copy)
                    act.activation(k.UT[:, :, bass.ds(m * TR, TR)], p, ACT.Copy).then_inc(tr_free, 1)

            pairs(act, NG, copy_out)

        @block.gpsimd
        def _(pool):
            pool.memset(k.ident[:, :], 0.0)
            pool.memset(k.ones[:, :], 1.0).then_inc(k.consts, 1)
            pool.memset(k.eps[:, :], EPS).then_inc(k.consts, 1)
            pool.memset(k.hmask[:, :], SW).then_inc(k.consts, 1)
            pool.iota(k.iota[:, :], [[1, WIN]], base=0, channel_multiplier=0,
                      allow_small_or_imprecise_dtypes=True).then_inc(k.consts, 1)
            pool.memset(k.src[:, NB:NB + 2, :], 0).then_inc(seen_out, 1)
            pool.memset(k.UT[:, :, N:N + WIN], 0.0).then_inc(seen_out, 1)
            pool.drain()
            pool.affine_select(out=k.ident[:, :], in_=k.ident[:, :], compare_op=ALU.not_equal, fill=1.0,
                               base=0, pattern=[[-1, 128]], channel_multiplier=1).then_inc(k.consts, 1)
            pool.affine_select(out=k.hmask[:, :], in_=k.hmask[:, :], compare_op=ALU.is_ge, fill=0.0,
                               base=-(128 - TAIL), pattern=[[0, 1]], channel_multiplier=1).then_inc(k.consts, 1)
            pool.wait_ge(prep_v, 2)
            pool.affine_select(out=k.dstl[:, NB - 1, :], in_=k.dstl[:, NB - 1, :], compare_op=ALU.is_ge, fill=0.5,
                               base=-SEEN, pattern=[[1, EK]], channel_multiplier=EK).then_inc(seen_out, 1)

            def store(n, h):
                pool.wait_ge(k.consts, k.CONST)
                pool.wait_ge(xn_done, n + 1)
                pool.dma_start(k.xn_d[bass.ds(n * (G * TR), G * TR), :].rearrange("(g p) c -> p g c", g=G),
                               XN[h][:, :, :]).then_inc(xn_st[h], 16)

            pairs(pool, NG, store)
            for h in range(2):
                pool.wait_ge(xn_st[h], 16 * (NG // 2))

        @block.vector
        def _(dve):
            dve.sem_inc(x_free, 2)
            dve.sem_inc(tr_free, G)
            dve.wait_ge(k.consts, k.CONST)
            dve.wait_ge(tab_in, TAB)
            dve.tensor_copy(basef[:, :], k.basei[:, :]).then_inc(prep_v, 1)
            for j in range(2):
                for b in range(CB):
                    dve.tensor_reduce(msum[:, j, b:b + 1], k.wqkv[:, b, j * C:(j + 1) * C], AX.X, ALU.add)
                dve.tensor_reduce(msum[:, j, CB:CB + 1], bq_row[:, j * C:(j + 1) * C], AX.X, ALU.add)
            for b in range(CB):
                dve.tensor_scalar(bv_wide[:, b, :], k.ones[:, :], bv_col[:, b:b + 1], None, ALU.mult)
            dve.drain()
            dve.tensor_scalar(msum[:, :, :], msum[:, :, :], 1.0 / C, None, ALU.mult)
            dve.drain()
            for j in range(2):
                for b in range(CB):
                    w = k.wqkv[:, b, j * C:(j + 1) * C]
                    dve.tensor_scalar(w, w, msum[:, j, b:b + 1], None, ALU.subtract)
            dve.tensor_scalar(k.bq[:, :], k.bq[:, :], msum[:, 0, CB:CB + 1], None, ALU.subtract)
            dve.tensor_scalar(k.bkv[:, 0:C], bq_row[:, C:2 * C], msum[:, 1, CB:CB + 1], None, ALU.subtract)
            dve.tensor_copy(k.bkv[:, C:2 * C], bq_row[:, 2 * C:3 * C])
            dve.wait_ge(base_full, 1)
            dve.tensor_copy(k.dstl[:, :, :], dsti[:, :, :])
            dve.drain()
            dve.tensor_tensor(k.dstl[:, :, :], k.dstl[:, :, :],
                              bank[5][:, 0:NB].unsqueeze(2).to_broadcast([128, NB, EK]), ALU.subtract).then_inc(prep_v, 1)
            dve.wait_ge(prep_p, 1)
            dve.tensor_copy(wvT[:, :, :], bank[6][:, :].rearrange("p (b c) -> p b c", b=CB)).then_inc(prep_v, 1)
            dve.tensor_copy(k.rwT[:, :, :], bank[7][:, 0:CB * NX].rearrange("p (b c) -> p b c", b=CB)).then_inc(prep_v, 1)
            dve.wait_ge(prep_p, 2)
            dve.tensor_copy(k.vwi[:, :, :], bank[6][:, :].rearrange("p (b c) -> p b c", b=CB))
            dve.tensor_tensor(k.bb[:, :], bank[7][:, 0:C], b_out_row[:, :], ALU.add)
            dve.drain()
            for b in range(CB):
                d = k.vwi[:, b, b * 128:(b + 1) * 128]
                dve.tensor_tensor(d, d, k.ident[:, :], ALU.add)

            def norm(n, h):
                dve.wait_ge(k.consts, k.CONST)
                dve.wait_ge(x_in[h], (n - h) * 8 + 16)
                for g in range(G):
                    dve.bn_stats(stats[:, g, :], X[h][:, g, :])
                dve.drain()
                for g in range(G):
                    dve.bn_aggr(mv[:, g, :], stats[:, g, :])
                dve.drain()
                dve.sem_inc(var_done, 1)
                dve.wait_ge(k.consts, k.CONST)
                dve.wait_ge(std_done, n + 1)
                dve.reciprocal(rstd[:, :], std[:, :])
                dve.drain()
                if not first_two(n):
                    dve.wait_ge(xn_st[h], (n - h) * 8)
                    dve.wait_ge(tr_free, n * G)
                for g in range(G):
                    last = dve.tensor_scalar(XN[h][:, g, :], X[h][:, g, :], mv[:, g, 0:1], rstd[:, g:g + 1],
                                             ALU.subtract, ALU.mult)
                last.then_inc(xn_done, 1)
                dve.drain()
                dve.sem_inc(x_free, 1)

            pairs(dve, NG, norm)

        @block.tensor
        def _(pe):
            pe.wait_ge(k.consts, k.CONST)
            pe.wait_ge(prep_v, 1)
            pe.matmul(bank[5][:, 0:NB], k.ones[0:1, :], basef[:, :], start=True, stop=True).then_inc(base_full, 1)
            pe.wait_ge(tab_in, TAB)
            for b in range(CB):
                for c in range(CB):
                    pe.transpose(bank[6][:, c * C + b * 128:c * C + (b + 1) * 128],
                                 k.wqkv[:, b, 2 * C + c * 128:2 * C + (c + 1) * 128], k.ident[:, :])
                last = pe.transpose(bank[7][:, b * NX:(b + 1) * NX], rw[:, b * 128:(b + 1) * 128], k.ident[0:NX, 0:NX])
            last.then_inc(prep_p, 1)
            pe.wait_ge(prep_v, 4)
            for b in range(CB):
                for c in range(CB):
                    pe.matmul(bank[6][:, b * C:(b + 1) * C], wvT[:, c, b * 128:(b + 1) * 128], k.wout[:, c, :],
                              start=c == 0, stop=c == CB - 1)
            for c in range(CB):
                last = pe.matmul(bank[7][:, 0:C], bv_wide[:, c, :], k.wout[:, c, :], start=c == 0, stop=c == CB - 1)
            last.then_inc(prep_p, 1)

            def turn(n, h):
                pe.wait_ge(xn_done, n + 1)
                for g in range(G):
                    pe.wait_ge(tr_free, n * G + g + 1)
                    for b in range(CB):
                        last = pe.transpose(bank[g][:, b * TR:(b + 1) * TR], XN[h][:, g, b * 128:(b + 1) * 128],
                                            k.ident[0:TR, 0:TR])
                    last.then_inc(tr_full, 1)

            pairs(pe, NG, turn)


def edge_mix_stage(k, st):
    nc, sb, sem, A = k.nc, k.sb, k.sem, k.A
    two = range(2)
    EA = [sb(f"edge_attr{h}", [128, EK, C], F32, st) for h in two]
    GA = [sb(f"gathered{h}", [128, EK, C], F32, st) for h in two]
    MSG = [sb(f"message{h}", [128, EK, C], F32, st) for h in two]
    IDX = [sb(f"src_index{h}", [128, EK], I32, st) for h in two]
    SEL = [sb(f"dst_select{h}", [128, EK, WIN], F32, st) for h in two]
    STG = [sb(f"xnT_tile{h}", [128, CB, TR], F32, st) for h in two]
    KV = [sb(f"key_value{h}", [TR, 2 * C], F32, st) for h in two]
    K2 = [sb(f"key_squared{h}", [TR, C], F32, st) for h in two]
    K4 = [sb(f"key_fourth{h}", [TR, C], F32, st) for h in two]
    VS = [sb(f"value_scaled{h}", [TR, C], F32, st) for h in two]
    KS = [sb(f"key_sum{h}", [TR, 1], F32, st) for h in two]
    RS = [sb(f"key_scale{h}", [TR, 1], F32, st) for h in two]
    Q2 = [sb(f"query_squared{h}", [128, CB, TR], F32, st) for h in two]
    Q4 = [sb(f"query_fourth{h}", [128, CB, TR], F32, st) for h in two]
    XT = [sb(f"x_tile{h}", [TR, C], F32, st) for h in two]
    RT = [sb(f"residual_tile{h}", [TR, C], F32, st) for h in two]
    KWX = sb("kv_out_weights", [128, CB, C + 1], F32, st)
    kvT = sb("kvT", [128, CB, C], F32, st)
    knorm = sb("key_norms", [128, CB], F32, st)
    qs = sb("query_scales", [TR, 4], F32, st)
    zero = sb("zero_row", [128, 2 * C], F32, st)
    PE_, KVP, KVT, NRM = k.psum[0:2], k.psum[2:4], k.psum[6], k.psum[7]
    QP, VP, TP = k.psum[2:4], k.psum[4:6], k.psum[6:8]
    gathers_begun = sem("gathers_begun")
    ea_in = [sem(f"edge_attr_in{h}") for h in two]
    g_in = [sem(f"gathered_in{h}") for h in two]
    stg_in = [sem(f"xnT_tile_in{h}") for h in two]
    xt_in = [sem(f"x_tile_in{h}") for h in two]
    r_out = [sem(f"residual_out{h}") for h in two]
    added, idx_ready, relu_done, sel_done = sem("edges_added"), sem("index_ready"), sem("relu_done"), sem("select_done")
    win_full, win_free = sem("window_full"), sem("window_free")
    kvp_full = sem("kv_psum_full")
    kv_done, ks_done, rs_done, k4_done, vs_done, kv_used = (sem(n) for n in (
        "key_value_done", "key_sum_done", "key_scale_done", "key_fourth_done", "value_scaled_done", "kv_used"))
    kvt_copied, kvt_scaled, norm_std, kw_full = sem("kvT_copied"), sem("kw_ready"), sem("key_norm_ready"), sem("kw_full")
    q_full, q_done, v_full, t_full, q_std, r_done, qs_sum, ready = (sem(n) for n in (
        "query_full", "query_done", "value_out_full", "mix_full", "query_norm_ready", "residual_done", "query_sums_done", "edge_stage_ready"))
    READY = 2

    def schedule(body):
        body(0, 1, 0, True)
        with body.eng.Fori(1, NT // 2) as i:
            body(i, 1, i * 2, False)
        body(NT // 2, None, None, False)
        body(NT // 2 + 1, 2, 0, True)
        body(NT // 2 + 2, 2, 2, False)
        with body.eng.Fori(NT // 2 + 3, NT + 1) as i:
            body(i, 2, i * 2 - (NT + 2), False)
        body(NT + 1, 3, None, False)

    def on(eng):
        def wrap(f):
            f.eng = eng
            schedule(f)
            return f
        return wrap

    def held(eng):
        eng.wait_ge(ready, READY)

    with nc.Block() as block:
        @block.sync
        def _(sp):
            @on(sp)
            def _(i, mix, t0, first):
                for h in two:
                    b = i * 2 + h
                    sp.wait_ge(added, b + 1)
                    lo = LAST if isinstance(b, int) and b == NB - 1 else b * EB
                    sp.dma_start(EA[h][:, :, :], A["edge_attr_256"][bass.ds(lo, EB), :]
                                 .rearrange("(p k) c -> p k c", k=EK)).then_inc(ea_in[h], 16)
                    if mix in (1, 2):
                        t = t0 + h
                        if mix == 2 and first:
                            sp.wait_ge(kvp_full, NT + 2)
                        sp.wait_ge(kvp_full if mix == 1 else v_full, t + 1)
                        sp.dma_start(STG[h][:, :, :], k.XNT[:, :, bass.ds(t * TR, TR)]).then_inc(stg_in[h], 16)
                    if mix == 2:
                        sp.wait_ge(r_done, t + 1)
                        sp.dma_start(XT[h][:, :], A["x"][bass.ds(t * TR, TR), :]).then_inc(xt_in[h], 16)
                        if not first:
                            sp.dma_start(k.r_d[bass.ds(t * TR - 2 * TR, TR), :], RT[h][:, :]).then_inc(r_out[h], 16)
                    if mix == 3:
                        t = NT - 2 + h
                        sp.wait_ge(r_done, t + 3)
                        sp.dma_start(k.r_d[bass.ds(t * TR, TR), :], RT[h][:, :]).then_inc(r_out[h], 16)
            for h in two:
                sp.wait_ge(r_out[h], 16 * (NT // 2))

        @block.gpsimd
        def _(pool):
            @on(pool)
            def _(i, mix, t0, first):
                for h in two:
                    b = i * 2 + h
                    pool.wait_ge(idx_ready, b + 1)
                    pool.wait_ge(added, b + 1)
                    pool.sem_inc(gathers_begun, 1)
                    for e in range(EK):
                        pool.indirect_dma_start(
                            out=GA[h][:, e, :], out_offset=None, in_=k.xn_d[:, :],
                            in_offset=bass.IndirectOffsetOnAxis(ap=IDX[h][:, e:e + 1], axis=0)).then_inc(g_in[h], 16)

        @block.vector
        def _(dve):
            dve.memset(zero[:, :], 0.0).then_inc(ready, 1)
            dve.memset(KWX[:, :, C:C + 1], 1.0).then_inc(ready, 1)
            for s, n in ((added, 2), (win_free, 2), (kvp_full, 2), (v_full, 2), (kv_done, 2), (kv_used, 2), (r_done, 2)):
                dve.sem_inc(s, n)
            for h in two:
                dve.tensor_copy(IDX[h][:, :], k.src[:, h, :]).then_inc(idx_ready, 1)

            def to_window(b, h):
                dve.wait_ge(win_full, b + 1)
                dve.wait_ge(win_free, b + 2)
                base = dve.value_load(k.basei[0:1, bass.ds(b, 1)], min_val=0, max_val=N - 1)
                w = k.UT[:, :, bass.ds(base, WIN)]
                dve.tensor_tensor(w, w, PE_[h][:, 0:CB * WIN].rearrange("p (b n) -> p b n", b=CB), ALU.add)\
                    .then_inc(win_free, 1)

            def kv_scale(t, h):
                dve.wait_ge(ks_done, t + 1)
                dve.wait_ge(kv_used, t + 1)
                dve.tensor_scalar(RS[h][:, :], KS[h][:, :], EPS_DIV, None, ALU.add)
                dve.drain()
                dve.reciprocal(RS[h][:, :], RS[h][:, :]).then_inc(rs_done, 1)
                dve.drain()
                dve.tensor_scalar(VS[h][:, :], KV[h][:, C:2 * C], RS[h][:, :], None, ALU.mult).then_inc(vs_done, 1)

            def mix_sums(t, h):
                dve.wait_ge(t_full, t + 1)
                dve.tensor_scalar(qs[:, 0:2], TP[h][0:TR, C:C + 2], 0.0, None, ALU.add).then_inc(qs_sum, 1)
                dve.drain()

            def mix_out(t, h):
                dve.tensor_scalar(qs[:, 2:3], qs[:, 0:1], EPS_DIV, None, ALU.add)
                dve.drain()
                dve.reciprocal(qs[:, 2:3], qs[:, 2:3])
                dve.drain()
                dve.wait_ge(q_std, t + 1)
                dve.tensor_scalar(qs[:, 3:4], qs[:, 3:4], qs[:, 2:3], EPS_NORM, ALU.mult, ALU.max)
                dve.drain()
                dve.reciprocal(qs[:, 3:4], qs[:, 3:4])
                dve.drain()
                dve.tensor_scalar(qs[:, 2:3], qs[:, 2:3], qs[:, 3:4], 1.0 / math.sqrt(N), ALU.mult, ALU.mult)
                dve.drain()
                if not first_two(t):
                    dve.wait_ge(r_out[h], (t - h) * 8)
                dve.wait_ge(xt_in[h], (t - h) * 8 + 16)
                dve.scalar_tensor_tensor(RT[h][:, :], TP[h][0:TR, 0:C], qs[:, 2:3], XT[h][:, :], ALU.mult, ALU.add)
                dve.drain()
                dve.tensor_tensor(RT[h][:, :], RT[h][:, :], VP[h][0:TR, 0:C], ALU.add)
                dve.drain()
                dve.tensor_tensor(RT[h][:, :], RT[h][:, :], k.bb[0:TR, :], ALU.add).then_inc(r_done, 1)
                dve.drain()

            @on(dve)
            def _(i, mix, t0, first):
                for h in two:
                    b = i * 2 + h
                    dve.wait_ge(ea_in[h], i * 16 + 16)
                    dve.wait_ge(g_in[h], i * (16 * EK) + 16 * EK)
                    dve.wait_ge(win_full, b - 1) if not (isinstance(b, int) and b < 2) else None
                    dve.tensor_tensor(MSG[h][:, :, :], GA[h][:, :, :], EA[h][:, :, :], ALU.add).then_inc(added, 1)
                    dve.tensor_copy(IDX[h][:, :], k.src[:, bass.ds(b + 2, 1), :].rearrange("p a k -> p (a k)")).then_inc(idx_ready, 1)
                    for e in range(EK):
                        last = dve.tensor_scalar(SEL[h][:, e, :], k.iota[:, :],
                                                 k.dstl[:, bass.ds(b, 1), e:e + 1].rearrange("p a k -> p (a k)"), None, ALU.is_equal)
                    last.then_inc(sel_done, 1)
                    if not (isinstance(b, int) and b == 0):
                        to_window(b - 1, 1 - h)
                    if mix == 1:
                        t = t0 + h
                        dve.wait_ge(kvp_full, t + 3)
                        dve.wait_ge(kv_used, t + 1)
                        dve.tensor_tensor(KV[h][:, :], KVP[h][0:TR, :], k.bkv[0:TR, :], ALU.add).then_inc(kv_done, 1)
                        kv_scale(t, h)
                    if mix is None and h == 0:
                        dve.wait_ge(kv_used, NT + 2)
                        dve.tensor_copy(kvT[:, :, :], KVT[:, :].rearrange("p (b c) -> p b c", b=CB)).then_inc(kvt_copied, 1)
                        dve.wait_ge(norm_std, 1)
                        dve.tensor_scalar(knorm[:, :], knorm[:, :], EPS_NORM, None, ALU.max)
                        dve.drain()
                        dve.reciprocal(knorm[:, :], knorm[:, :])
                        dve.drain()
                        dve.wait_ge(kw_full, 1)
                        for c in range(CB):
                            last = dve.tensor_scalar(KWX[:, c, 0:C], KVT[:, c * C:(c + 1) * C], knorm[:, c:c + 1], None, ALU.mult)
                        last.then_inc(kvt_scaled, 1)
                    if mix == 2 and not (first and h == 0):
                        mix_sums(t0 + h - 1, 1 - h)
                        mix_out(t0 + h - 1, 1 - h)
                    if mix == 3 and h == 0:
                        mix_sums(NT - 1, 1)
                        mix_out(NT - 1, 1)
            to_window(NB - 1, 1)

        @block.scalar
        def _(act):
            @on(act)
            def _(i, mix, t0, first):
                for h in two:
                    b = i * 2 + h
                    act.wait_ge(added, b + 3)
                    act.activation(MSG[h][:, :, :], MSG[h][:, :, :], ACT.Relu).then_inc(relu_done, 1)
                    if mix == 1:
                        t = t0 + h
                        act.wait_ge(kv_done, t + 3)
                        act.activation(K2[h][:, :], KV[h][:, 0:C], ACT.Square, accum_out=KS[h][:, :]).then_inc(ks_done, 1)
                        act.drain()
                        act.wait_ge(rs_done, t + 1)
                        act.activation(K4[h][:, :], K2[h][:, :], ACT.Square, scale=RS[h][:, :]).then_inc(k4_done, 1)
                    if mix is None and h == 0:
                        act.wait_ge(kv_used, NT + 2)
                        act.activation(knorm[:, :], NRM[:, 0:CB], ACT.Sqrt).then_inc(norm_std, 1)
                    if mix == 2:
                        t = t0 + h
                        if not (first and h == 0):
                            act.wait_ge(qs_sum, t)
                            act.activation(qs[:, 3:4], qs[:, 1:2], ACT.Sqrt).then_inc(q_std, 1)
                        act.drain()
                        act.wait_ge(q_full, t + 1)
                        for c in range(CB):
                            act.activation(Q2[h][:, c, :], QP[h][:, c * TR:(c + 1) * TR], ACT.Square, bias=k.bq[:, c:c + 1])
                        act.drain()
                        act.activation(Q4[h][:, :, :], Q2[h][:, :, :], ACT.Square).then_inc(q_done, 1)
                    if mix == 3 and h == 0:
                        act.wait_ge(qs_sum, NT)
                        act.activation(qs[:, 3:4], qs[:, 1:2], ACT.Sqrt).then_inc(q_std, 1)

        @block.tensor
        def _(pe):
            held(pe)
            pe.matmul(KVT[:, :], zero[:, 0:128], zero[:, :], start=True, stop=False, skip_group_check=True)
            pe.matmul(NRM[:, 0:CB], zero[:, 0:128], zero[:, 0:CB], start=True, stop=False, skip_group_check=True)

            def kv_sums(t, h, done=False):
                held(pe)
                pe.wait_ge(k4_done, t + 1)
                pe.wait_ge(vs_done, t + 1)
                for c in range(CB):
                    pe.matmul(KVT[:, c * C:(c + 1) * C], VS[h][:, c * 128:(c + 1) * 128], K2[h][:, :],
                              start=False, stop=done, skip_group_check=True)
                for c in range(CB):
                    last = pe.matmul(NRM[:, c:c + 1], K4[h][:, c * 128:(c + 1) * 128], k.ones[0:TR, 0:1],
                                     start=False, stop=done, skip_group_check=True)
                last.then_inc(kv_used, 1)

            def mixed(t, h):
                held(pe)
                pe.wait_ge(q_done, t + 1)
                pe.wait_ge(r_done, t + 1)
                for c in range(CB):
                    pe.matmul(TP[h][0:TR, 0:C + 1], Q2[h][:, c, :], KWX[:, c, :], start=c == 0, stop=c == CB - 1)
                for c in range(CB):
                    last = pe.matmul(TP[h][0:TR, C + 1:C + 2], Q4[h][:, c, :], k.ones[:, 0:1], start=c == 0, stop=c == CB - 1)
                last.then_inc(t_full, 1)

            @on(pe)
            def _(i, mix, t0, first):
                for h in two:
                    b = i * 2 + h
                    if mix == 1 and not (first and h == 0):
                        kv_sums(t0 + h - 1, 1 - h)
                    if mix is None and h == 0:
                        kv_sums(NT - 1, 1, True)
                        pe.wait_ge(kvt_copied, 1)
                        pe.wait_ge(norm_std, 1)
                        for q in range(CB):
                            for c in range(CB):
                                last = pe.matmul(KVT[:, q * C:(q + 1) * C], kvT[:, c, q * 128:(q + 1) * 128], k.wout[:, c, :],
                                                 start=c == 0, stop=c == CB - 1)
                        last.then_inc(kw_full, 1)
                        pe.wait_ge(kvt_scaled, 1)
                    if mix == 2 and not (first and h == 0):
                        mixed(t0 + h - 1, 1 - h)
                    if mix == 3 and h == 0:
                        mixed(NT - 1, 1)
                    if mix in (1, 2):
                        t = t0 + h
                        pe.wait_ge(stg_in[h], ((t - h) * 8 + 16) + (mix - 1) * (8 * NT))
                    if mix == 1:
                        held(pe)
                        pe.wait_ge(kv_done, t + 1)
                        for c in range(CB):
                            last = pe.matmul(KVP[h][0:TR, :], STG[h][:, c, :], k.wqkv[:, c, C:3 * C], start=c == 0, stop=c == CB - 1)
                        last.then_inc(kvp_full, 1)
                    if mix == 2:
                        held(pe)
                        pe.wait_ge(r_done, t + 1)
                        if not (first):
                            pe.wait_ge(q_done, t - 1)
                        for q in range(CB):
                            for c in range(CB):
                                last = pe.matmul(QP[h][:, q * TR:(q + 1) * TR], k.wqkv[:, c, q * 128:(q + 1) * 128], STG[h][:, c, :],
                                                 start=c == 0, stop=c == CB - 1)
                        last.then_inc(q_full, 1)
                        for c in range(CB):
                            last = pe.matmul(VP[h][0:TR, 0:C], STG[h][:, c, :], k.vwi[:, c, :], start=c == 0, stop=c == CB - 1)
                        last.then_inc(v_full, 1)
                    held(pe)
                    pe.wait_ge(relu_done, b + 1)
                    pe.wait_ge(sel_done, b + 1)
                    pe.wait_ge(win_free, b + 1)
                    for c in range(CB):
                        for e in range(EK):
                            last = pe.matmul(PE_[h][:, c * WIN:(c + 1) * WIN], MSG[h][:, e, c * 128:(c + 1) * 128], SEL[h][:, e, :],
                                             start=e == 0, stop=e == EK - 1)
                    last.then_inc(win_full, 1)


def gnn_mlp_stage(k, st):
    nc, sb, sem, A = k.nc, k.sb, k.sem, k.A
    W1 = sb("w1_gnn", [128, CB, HID], F32, st)
    W2 = sb("w2_gnn", [128, FB, C], F32, st)
    cols = sb("hidden_columns", [128, 3, FB], F32, st)
    outs = sb("out_columns", [128, 6, CB], F32, st)
    HT = sb("hiddenT", [128, FB, N], F32, st)
    ACTV = [sb(f"activated{h}", [128, FB, CH], F32, st) for h in range(2)]
    hst = sb("hidden_stats", [128, FB, NC, 6], F32, st)
    ost = sb("out_stats", [128, CB, NC, 6], F32, st)
    hmv = sb("hidden_mv", [128, FB, 2], F32, st)
    omv = sb("out_mv", [128, CB, 2], F32, st)
    sc = sb("hidden_scale", [128, 2, FB], F32, st)
    tmp = sb("graph_terms", [128, 8, CB], F32, st)
    gs = sb("graph_sums", [128, 6], F32, st)
    fill = sb("empty_row", [128, ROW], F32, st)
    w_in, col_in = sem("gnn_weights_in"), sem("gnn_columns_in")
    h_full, h_used, h_seen = sem("hidden_full"), sem("hidden_copied"), sem("hidden_seen")
    std_in, std_out, sc_done = sem("bn_var_ready"), sem("bn_std_ready"), sem("bn_scale_ready")
    a_done, o_full, o_used = sem("activated_done"), sem("out_full"), sem("out_copied")
    gsum_in, gsum_out, empty, empty_out = sem("graph_sum_in"), sem("graph_sum_out"), sem("empty_row_ready"), sem("empty_rows_out")
    HP = [k.psum[0:2], k.psum[2:4]]
    OP = k.psum[4:6]
    GP = k.psum[6]

    with nc.Block() as block:
        @block.sync
        def _(sp):
            sp.dma_start(W1[:, :, :], A["L0_gnn_W1"].rearrange("(b p) n -> p b n", p=128)).then_inc(w_in, 16)
            sp.dma_start(W2[:, :, :], A["L0_gnn_W2"].rearrange("(b p) n -> p b n", p=128)).then_inc(w_in, 16)
            with nc.allow_non_contiguous_dma("one word a partition"):
                for i, name in enumerate(("L0_gnn_b1", "L0_gnn_bn_gamma", "L0_gnn_bn_beta")):
                    sp.dma_start(cols[:, i, :], A[name].rearrange("(b p) -> p b", p=128)).then_inc(col_in, 16)
                for i, name in enumerate(("L0_gnn_b2", "L0_gnn_ln_w", "L0_gnn_ln_b", "L0_gnn_gn_w", "L0_gnn_gn_b", "L0_gnn_gn_ms")):
                    sp.dma_start(outs[:, i, :], A[name].rearrange("(b p) -> p b", p=128)).then_inc(col_in, 16)
            sp.wait_ge(empty, 3)
            sp.dma_start(k.disp_d.rearrange("(i p) c -> p i c", p=128),
                         fill[:, :].unsqueeze(1).to_broadcast([128, FT + 1, ROW])).then_inc(empty_out, 16)
            sp.dma_start(k.acc_d[N:N + 128, :], fill[:, 0:C]).then_inc(empty_out, 16)
            sp.wait_ge(empty_out, 32)

        @block.gpsimd
        def _(pool):
            pool.memset(fill[:, 0:ROW - 1], 0.0).then_inc(empty, 1)
            pool.iota(fill[:, ROW - 1:ROW].bitcast(I32), [[0, 1]], base=N, channel_multiplier=1).then_inc(empty, 1)
            pool.drain().then_inc(empty, 1)

        @block.tensor
        def _(pe):
            pe.wait_ge(w_in, 32)

            def up(c, h):
                if not (isinstance(c, int) and c < 2):
                    pe.wait_ge(h_used, c + 1)
                else:
                    pe.wait_ge(h_used, c + 1)
                for f in range(FB):
                    for b in range(CB):
                        last = pe.matmul(HP[h][f // 2][:, (f % 2) * CH:(f % 2 + 1) * CH], W1[:, b, f * 128:(f + 1) * 128],
                                         k.UT[:, b, bass.ds(c * CH, CH)], start=b == 0, stop=b == CB - 1)
                last.then_inc(h_full, 1)

            pairs(pe, NC, up)

            def down(c, h):
                pe.wait_ge(a_done, c + 1)
                pe.wait_ge(o_used, c + 1)
                for q in range(CB):
                    for f in range(FB):
                        last = pe.matmul(OP[h][:, q * CH:(q + 1) * CH], W2[:, f, q * 128:(q + 1) * 128], ACTV[h][:, f, :],
                                         start=f == 0, stop=f == FB - 1)
                last.then_inc(o_full, 1)

            pairs(pe, NC, down)
            for n, w in ((0, 2), (1, 2)):
                pe.wait_ge(gsum_in, n + 1)
                pe.matmul(GP[:, n * 2:n * 2 + w], k.ones[:, :], tmp[:, n, 0:w], start=True, stop=True).then_inc(gsum_out, 1)

        @block.scalar
        def _(act):
            act.wait_ge(col_in, 16 * 9)

            def copy_out(c, h):
                act.wait_ge(h_full, c + 1)
                for f in range(FB):
                    last = act.activation(HT[:, f, bass.ds(c * CH, CH)], HP[h][f // 2][:, (f % 2) * CH:(f % 2 + 1) * CH],
                                          ACT.Identity, bias=cols[:, 0, f:f + 1])
                last.then_inc(h_used, 1)

            act.sem_inc(h_used, 2)
            pairs(act, NC, copy_out)
            act.wait_ge(std_in, 1)
            act.activation(sc[:, 0, :], hmv[:, :, 1], ACT.Sqrt, bias=k.eps[:, :]).then_inc(std_out, 1)
            act.wait_ge(sc_done, 1)

            def activate(c, h):
                if not (isinstance(c, int) and c < 2):
                    act.wait_ge(o_full, c - 1)
                else:
                    act.wait_ge(h_used, 2)
                for f in range(FB):
                    last = act.activation(ACTV[h][:, f, :], HT[:, f, bass.ds(c * CH, CH)], ACT.Relu,
                                          scale=sc[:, 0, f:f + 1], bias=sc[:, 1, f:f + 1])
                last.then_inc(a_done, 1)

            activate(0, 0)
            activate(1, 1)
            with act.Fori(1, NC // 2) as i:
                activate(i * 2, 0)
                activate(i * 2 + 1, 1)
            activate(NC - 1, 0)
            act.wait_ge(std_in, 2)
            act.activation(tmp[:, 2, 0:1], tmp[:, 2, 0:1], ACT.Sqrt, bias=k.eps[:, :]).then_inc(std_out, 1)
            act.wait_ge(std_in, 3)
            act.activation(tmp[:, 6, :], tmp[:, 6, :], ACT.Sqrt, bias=k.eps[:, :]).then_inc(std_out, 1)

        @block.vector
        def _(dve):
            def seen(c, h):
                dve.wait_ge(h_used, c + 3)
                for f in range(FB):
                    dve.bn_stats(hst[:, f, bass.ds(c, 1), :].rearrange("p a s -> p (a s)"), HT[:, f, bass.ds(c * CH, CH)])

            pairs(dve, NC, seen)
            dve.drain()
            for f in range(FB):
                dve.bn_aggr(hmv[:, f, :], hst[:, f, :, :])
            dve.drain()
            dve.sem_inc(std_in, 1)
            dve.wait_ge(std_out, 1)
            dve.reciprocal(sc[:, 0, :], sc[:, 0, :])
            dve.drain()
            dve.wait_ge(col_in, 16 * 9)
            dve.tensor_tensor(sc[:, 0, :], sc[:, 0, :], cols[:, 1, :], ALU.mult)
            dve.drain()
            dve.tensor_tensor(sc[:, 1, :], hmv[:, :, 0], sc[:, 0, :], ALU.mult)
            dve.drain()
            dve.tensor_tensor(sc[:, 1, :], cols[:, 2, :], sc[:, 1, :], ALU.subtract).then_inc(sc_done, 1)
            dve.sem_inc(o_used, 2)

            def copy_out(c, h):
                dve.wait_ge(o_full, c + 1)
                for q in range(CB):
                    dve.bn_stats(ost[:, q, bass.ds(c, 1), :].rearrange("p a s -> p (a s)"), OP[h][:, q * CH:(q + 1) * CH])
                for q in range(CB):
                    last = dve.tensor_scalar(k.UT[:, q, bass.ds(c * CH, CH)], OP[h][:, q * CH:(q + 1) * CH],
                                             outs[:, 0, q:q + 1], None, ALU.add)
                last.then_inc(o_used, 1)

            pairs(dve, NC, copy_out)
            dve.drain()
            for q in range(CB):
                dve.bn_aggr(omv[:, q, :], ost[:, q, :, :])
            dve.drain()

            def step(ins):
                dve.drain()
                return ins

            b2, ln_w, ln_b, gn_w, gn_b, gn_ms = (outs[:, i, :] for i in range(6))
            mean, var = omv[:, :, 0], omv[:, :, 1]
            tt, ts = dve.tensor_tensor, dve.tensor_scalar
            tt(mean, mean, b2, ALU.add)
            dve.drain()
            dve.tensor_reduce(tmp[:, 0, 0:1], mean, AX.X, ALU.add)
            dve.memset(tmp[:, 0, 1:2], 0.0)
            dve.memset(tmp[:, 1, 1:2], 0.0)
            dve.drain()
            dve.sem_inc(gsum_in, 1)
            dve.wait_ge(gsum_out, 1)
            ts(gs[:, 0:1], GP[:, 0:1], 1.0 / C, None, ALU.mult)
            dve.drain()
            ts(tmp[:, 3, :], mean, gs[:, 0:1], None, ALU.subtract)
            dve.drain()
            tt(tmp[:, 3, :], tmp[:, 3, :], tmp[:, 3, :], ALU.mult)
            dve.drain()
            tt(tmp[:, 3, :], tmp[:, 3, :], var, ALU.add)
            dve.drain()
            dve.tensor_reduce(tmp[:, 1, 0:1], tmp[:, 3, :], AX.X, ALU.add)
            dve.drain()
            dve.sem_inc(gsum_in, 1)
            dve.wait_ge(gsum_out, 2)
            ts(tmp[:, 2, 0:1], GP[:, 2:3], 1.0 / C, None, ALU.mult)
            dve.drain()
            dve.sem_inc(std_in, 1)
            dve.wait_ge(std_out, 2)
            dve.reciprocal(gs[:, 1:2], tmp[:, 2, 0:1])
            dve.drain()
            ts(tmp[:, 3, :], ln_w, gs[:, 1:2], None, ALU.mult)
            dve.drain()
            ts(tmp[:, 4, :], tmp[:, 3, :], gs[:, 0:1], None, ALU.mult)
            tt(tmp[:, 5, :], tmp[:, 3, :], mean, ALU.mult)
            dve.drain()
            tt(tmp[:, 4, :], ln_b, tmp[:, 4, :], ALU.subtract)
            dve.drain()
            tt(tmp[:, 5, :], tmp[:, 5, :], tmp[:, 4, :], ALU.add)
            dve.drain()
            tt(tmp[:, 7, :], tmp[:, 5, :], gn_ms, ALU.mult)
            tt(tmp[:, 6, :], tmp[:, 3, :], tmp[:, 3, :], ALU.mult)
            dve.drain()
            tt(tmp[:, 5, :], tmp[:, 5, :], tmp[:, 7, :], ALU.subtract)
            tt(tmp[:, 6, :], tmp[:, 6, :], var, ALU.mult)
            dve.drain()
            tt(tmp[:, 5, :], tmp[:, 5, :], tmp[:, 5, :], ALU.mult)
            dve.drain()
            tt(tmp[:, 6, :], tmp[:, 6, :], tmp[:, 5, :], ALU.add)
            tt(tmp[:, 4, :], tmp[:, 4, :], tmp[:, 7, :], ALU.subtract)
            dve.drain()
            dve.sem_inc(std_in, 1)
            dve.wait_ge(std_out, 3)
            dve.reciprocal(tmp[:, 6, :], tmp[:, 6, :])
            dve.drain()
            tt(tmp[:, 6, :], tmp[:, 6, :], gn_w, ALU.mult)
            dve.drain()
            tt(k.gsc[:, :], tmp[:, 3, :], tmp[:, 6, :], ALU.mult)
            tt(k.gbi[:, :], tmp[:, 4, :], tmp[:, 6, :], ALU.mult)
            dve.drain()
            tt(k.gbi[:, :], k.gbi[:, :], gn_b, ALU.add)


def residual_stage(k, st):
    nc, sb, sem = k.nc, k.sb, k.sem
    G = 5
    NG = NT // G
    two = range(2)
    Z = [sb(f"activatedT{h}", [128, G, CB, TR], F32, st) for h in two]
    R = [sb(f"residual_in{h}", [TR, G, C], F32, st) for h in two]
    XN = [sb(f"tokens{h}", [TR, G, C], F32, st) for h in two]
    XT = [sb(f"tokensT{h}", [128, G, CB, TR], F32, st) for h in two]
    stats = sb("ln2_stats", [TR, G, 6], F32, st)
    mv = sb("ln2_mv", [TR, G, 2], F32, st)
    std = sb("ln2_std", [TR, G], F32, st)
    r_in = [sem(f"residual_rows_in{h}") for h in two]
    x1_out, tok_out = [sem(f"x1_out{h}") for h in two], [sem(f"token_rows_out{h}") for h in two]
    z_done, zt_full, x1_done, std_in, std_out, xn_done = (sem(n) for n in (
        "activatedT_done", "activated_rows_full", "x1_done", "ln2_var_ready", "ln2_std_ready", "tokens_done"))
    xt_full, xt_free, xt_done, lg_full, lg_done = (sem(n) for n in (
        "tokensT_full", "tokensT_free", "tokensT_done", "logits_full", "logits_done"))
    ZP, XP, LP = k.psum[0:3], k.psum[3:5], k.psum[5]
    zp = lambda g: ZP[g // 2][0:TR, (g % 2) * C:(g % 2 + 1) * C]

    with nc.Block() as block:
        @block.sync
        def _(sp):
            def move(n, h):
                rows = bass.ds(n * (G * TR), G * TR)
                if not first_two(n):
                    sp.wait_ge(x1_out[h], (n - h) * 8)
                    sp.wait_ge(tok_out[h], (n - h) * 8)
                sp.dma_start(R[h][:, :, :], k.r_d[rows, :].rearrange("(g p) c -> p g c", g=G)).then_inc(r_in[h], 16)

            pairs(sp, NG, move)

        @block.gpsimd
        def _(pool):
            def store(n, h):
                rows = bass.ds(n * (G * TR), G * TR)
                pool.wait_ge(x1_done, n + 1)
                pool.sem_inc(k.pool_turn, 1)
                pool.dma_start(k.acc_d[rows, :].rearrange("(g p) c -> p g c", g=G), R[h][:, :, :]).then_inc(x1_out[h], 16)
                pool.wait_ge(xn_done, n + 1)
                pool.sem_inc(k.pool_turn, 1)
                pool.dma_start(k.tok_d[rows, 0:C].rearrange("(g p) c -> p g c", g=G), XN[h][:, :, :]).then_inc(tok_out[h], 16)

            pairs(pool, NG, store)
            for h in two:
                pool.wait_ge(x1_out[h], NG * 8)
                pool.wait_ge(tok_out[h], NG * 8)

        @block.scalar
        def _(act):
            def activate(n, h):
                for g in range(G):
                    for b in range(CB):
                        last = act.activation(Z[h][:, g, b, :], k.UT[:, b, bass.ds(n * (G * TR) + g * TR, TR)], ACT.Relu,
                                              scale=k.gsc[:, b:b + 1], bias=k.gbi[:, b:b + 1])
                last.then_inc(z_done, 1)

            def rest(n, h, more):
                act.wait_ge(std_in, n + 1)
                act.activation(std[:, :], mv[:, :, 1], ACT.Sqrt, bias=k.eps[0:TR, :]).then_inc(std_out, 1)
                if more:
                    if not first_two(n):
                        act.wait_ge(zt_full, n)
                    elif n:
                        act.wait_ge(zt_full, 1)
                    activate(n + 1, 1 - h)
                for g in range(G):
                    act.wait_ge(xt_full, n * G + g + 1)
                    act.activation(XT[h][:, g, :, :], XP[g % 2][:, 0:CB * TR].rearrange("p (b n) -> p b n", b=CB),
                                   ACT.Copy).then_inc(xt_free, 1)
                act.wait_ge(lg_full, n + 1)
                act.activation(k.LG[:, bass.ds(n * G, G), :], LP[0:TR, 0:G * NX].rearrange("p (g e) -> p g e", g=G),
                               ACT.Copy).then_inc(lg_done, 1)

            act.sem_inc(xt_free, 2)
            act.sem_inc(lg_done, 1)
            activate(0, 0)
            rest(0, 0, True)
            rest(1, 1, True)
            with act.Fori(1, NG // 2 - 1) as i:
                for h in two:
                    rest(i * 2 + h, h, True)
            rest(NG - 2, 0, True)
            rest(NG - 1, 1, False)

        @block.tensor
        def _(pe):
            def turn(n, h):
                pe.wait_ge(z_done, n + 1)
                if not (isinstance(n, int) and n == 0):
                    pe.wait_ge(x1_done, n)
                for g in range(G):
                    for b in range(CB):
                        last = pe.transpose(zp(g)[:, b * 128:(b + 1) * 128], Z[h][:, g, b, :], k.ident[:, :])
                last.then_inc(zt_full, 1)

            def rest(n, h, more):
                if more:
                    turn(n + 1, 1 - h)
                pe.wait_ge(xn_done, n + 1)
                for g in range(G):
                    m = n * G + g
                    pe.wait_ge(xt_free, m + 1 if g else m + 2)
                    for b in range(CB):
                        last = pe.transpose(XP[g % 2][:, b * TR:(b + 1) * TR], XN[h][:, g, b * 128:(b + 1) * 128], k.ident[0:TR, 0:TR])
                    last.then_inc(xt_full, 1)
                pe.wait_ge(xt_free, n * G + G + 2)
                pe.wait_ge(lg_done, n + 1)
                for g in range(G):
                    for b in range(CB):
                        last = pe.matmul(LP[0:TR, g * NX:(g + 1) * NX], XT[h][:, g, b, :], k.rwT[:, b, :], start=b == 0, stop=b == CB - 1)
                last.then_inc(lg_full, 1)

            turn(0, 0)
            with pe.Fori(0, NG // 2 - 1) as i:
                for h in two:
                    rest(i * 2 + h, h, True)
            rest(NG - 2, 0, True)
            rest(NG - 1, 1, False)

        @block.vector
        def _(dve):
            def norm(n, h):
                dve.wait_ge(r_in[h], (n - h) * 8 + 16)
                dve.wait_ge(zt_full, n + 1)
                for z in range(0, G, 2):
                    w = min(2, G - z)
                    last = dve.tensor_tensor(R[h][:, z:z + w, :], R[h][:, z:z + w, :],
                                             ZP[z // 2][0:TR, 0:w * C].rearrange("p (g c) -> p g c", g=w), ALU.add)
                last.then_inc(x1_done, 1)
                dve.drain()
                for g in range(G):
                    dve.bn_stats(stats[:, g, :], R[h][:, g, :])
                dve.drain()
                for g in range(G):
                    dve.bn_aggr(mv[:, g, :], stats[:, g, :])
                dve.drain()
                dve.sem_inc(std_in, 1)
                dve.wait_ge(std_out, n + 1)
                dve.reciprocal(std[:, :], std[:, :])
                dve.drain()
                if not first_two(n):
                    dve.wait_ge(tok_out[h], (n - h) * 8)
                    dve.wait_ge(lg_done, n)
                for g in range(G):
                    last = dve.tensor_scalar(XN[h][:, g, :], R[h][:, g, :], mv[:, g, 0:1], std[:, g:g + 1], ALU.subtract, ALU.mult)
                last.then_inc(xn_done, 1)

            pairs(dve, NG, norm)


def moe_stage(k, st):
    W = k.sb("expert_weights", [128, NX, 2, WL], F16, st)
    te = k.sb("tile_expert", [1, FT + 1], I32, st)
    tef = k.sb("tile_expert_rows", [128, FT + 1], F32, st)
    with ExitStack() as low:
        dispatch_stage(k, low, W, te, tef)
    with ExitStack() as low:
        expert_stage(k, low, W, te, tef)


def hidden_start(j):
    return min(128 * j, H - 128)


def dispatch_stage(k, st, W, te, tef):
    nc, sb, sem, A = k.nc, k.sb, k.sem, k.A
    two = range(2)
    RAW = [sb(f"raw_weights{m}", [128, HB * C], F32, st) for m in range(3)]
    XS = [sb(f"rows_to_send{h}", [TR, 2, ROW], F32, st) for h in two]
    IX = [sb(f"send_index{h}", [TR, 2, 2], I32, st) for h in two]
    sh = [TR, NT, NX]
    T = lambda name, shape=sh, dt=F32: sb(name, shape, dt, st)
    prob, w1, w2, oh1, oh2, oh = (T(n) for n in ("probs", "rank1", "rank2", "choice1", "choice2", "chosen"))
    m1, m2, f1, f2, den = (T(n, [TR, NT]) for n in ("top1", "top2", "first1", "first2", "gate_sum"))
    run = [T(f"running{h}", [128, NT, NX]) for h in two]
    cnt = [T(f"expert_ends{h}", [128, NX]) for h in two]
    tiles, tilesi, base = T("expert_tiles", [128, NX]), T("expert_tiles_i", [128, NX], I32), T("expert_base", [128, NX])
    tri, iof, iot, back = T("earlier_partition", [TR, TR]), T("iota_tiles", [128, FT + 1]), T("tile_past", [128, FT + 1, NX]), T("back_rank", [TR, NX])
    pos, extra, ids = T("row_of_pair", [TR, NT, 2], I32), T("row_extras", [TR, NT, 4]), T("token_ids", [TR, NT], I32)
    posf = T("row_of_pair_f", [TR, NT, 2])
    raw_in = [sem(f"raw_weights_in{m}") for m in range(3)]
    wt_full, wt_hi, wt_lo = sem("weightsT_full"), sem("weights_high"), sem("weights_low")
    ready, shifted, exped, routed, ranks, extra_done, extra_out = (sem(n) for n in (
        "route_consts", "logits_shifted", "exp_done", "routed", "ranks_full", "extras_done", "extras_out"))
    xs_in, sent = [sem(f"rows_to_send_in{h}") for h in two], [sem(f"rows_sent{h}") for h in two]
    NS = NT // 2
    PB = [k.psum[0:3], k.psum[3:6]]
    part = lambda e, p, lo, n: W[:, bass.ds(e, 1), p:p + 1, lo:lo + n].rearrange("q a b n -> q (a b n)")
    part2 = lambda e, p, lo, n: W[:, bass.ds(e, 1), p:p + 1, lo:lo + 2 * H].rearrange("q a b (k h) -> q (a b k) h", k=2)[:, :, 0:n]

    def pieces(m, e, p):
        if m < 2:
            at = m * CB * H
            rest = lambda b: b[:, :].rearrange("p (k h) -> p k h", k=2)
            return [(0, lambda b: b[:, :], part(e, p, at, 512), False), (1, lambda b: b[:, :], part(e, p, at + H, 512), False),
                    (2, lambda b: rest(b)[:, :, 0:128], part2(e, p, at, H)[:, :, 512:640], False),
                    (2, lambda b: rest(b)[:, :, 256 - TAIL:256], part2(e, p, at, H)[:, :, 640:H], False)]
        at = 2 * CB * H
        return [(0, lambda b: b[:, :], part(e, p, at, 512), False), (1, lambda b: b[:, :], part(e, p, at + 512, 512), False),
                (2, lambda b: b[:, 0:C], part(e, p, at + 4 * C, C), False), (2, lambda b: b[:, C:2 * C], part(e, p, at + 5 * C, C), True)]

    def experts(eng, body):
        with eng.Fori(0, NX // 2) as i:
            for h in two:
                for m in range(3):
                    body(i * 2 + h, m, i * 6 + (3 * h + m), (3 * h + m) % 2)

    with nc.Block() as block:
        @block.sync
        def _(sp):
            def load(e, m, n, s):
                sp.wait_ge(wt_full, n + 1)
                if m < 2:
                    w = A[("L0_ffn_w1", "L0_ffn_w3")[m]][bass.ds(e, 1), :, :].rearrange("a h c -> (a h) c")
                    dst = RAW[m][:, :].rearrange("p (j c) -> p j c", c=C)
                    sp.dma_start(dst[:, 0:HB - 1, :], w[0:128 * (HB - 1), :].rearrange("(j p) c -> p j c", p=128)).then_inc(raw_in[m], 16)
                    sp.dma_start(dst[:, HB - 1, :], w[H - 128:H, :]).then_inc(raw_in[m], 16)
                else:
                    sp.dma_start(RAW[m][:, 0:CB * H].rearrange("p (b h) -> p b h", b=CB),
                                 A["L0_ffn_w2"][bass.ds(e, 1), :, :].rearrange("a (b p) h -> p (a b) h", p=128)).then_inc(raw_in[m], 16)

            experts(sp, load)

        @block.gpsimd
        def _(pool):
            pool.memset(tri[:, :], 1.0).then_inc(ready, 1)
            pool.iota(back[:, :], [[-1, NX]], base=NX, channel_multiplier=0, allow_small_or_imprecise_dtypes=True).then_inc(ready, 1)
            pool.iota(iof[:, :], [[1, FT + 1]], base=0, channel_multiplier=0, allow_small_or_imprecise_dtypes=True).then_inc(ready, 1)
            pool.iota(ids[:, :], [[TR, NT]], base=0, channel_multiplier=1).then_inc(ready, 1)
            pool.drain()
            pool.affine_select(out=tri[:, :], in_=tri[:, :], compare_op=ALU.is_gt, fill=0.0, base=0,
                               pattern=[[1, TR]], channel_multiplier=-1).then_inc(ready, 1)
            pool.wait_ge(routed, 1)

            def send(n, h):
                if not first_two(n):
                    pool.wait_ge(sent[h], (n - h) * 32)
                    pool.sem_inc(k.pool_turn, 1)
                pool.tensor_copy(IX[h][:, :, :], pos[:, bass.ds(n * 2, 2), :])
                pool.drain()
                pool.wait_ge(xs_in[h], (n - h) * 8 + 16)
                pool.sem_inc(k.pool_turn, 1)
                for t in two:
                    for c in two:
                        pool.indirect_dma_start(out=k.disp_d[:, :], out_offset=bass.IndirectOffsetOnAxis(ap=IX[h][:, t, c:c + 1], axis=0),
                                                in_=XS[h][:, t, :], in_offset=None).then_inc(sent[h], 16)

            pairs(pool, NS, send)
            for h in two:
                pool.wait_ge(sent[h], 64 * ((NS + 1 - h) // 2))

        @block.scalar
        def _(act):
            act.wait_ge(shifted, 1)
            act.activation(prob[:, :, :], prob[:, :, :], ACT.Exp).then_inc(exped, 1)
            with nc.allow_non_contiguous_dma("four words of each token"):
                act.wait_ge(extra_done, 1)
                act.dma_start(k.tok_d.rearrange("(t p) c -> p t c", p=TR)[:, :, C:ROW], extra[:, :, :]).then_inc(extra_out, 16)
            act.wait_ge(extra_out, 16)

            def high(e, m, n, s):
                act.wait_ge(wt_full, n + 4)
                for bank, cols, to, masked in pieces(m, e, 0):
                    scale = k.hmask[:, :] if masked else SW
                    last = act.activation(to, cols(PB[s][bank]), ACT.Copy, scale=scale)
                last.then_inc(wt_hi, 1)

            def load(n, h):
                if not first_two(n):
                    act.wait_ge(sent[h], (n - h) * 32)
                act.dma_start(XS[h][:, :, :], k.tok_d[bass.ds(n * (2 * TR), 2 * TR), :].rearrange("(t p) c -> p t c", t=2)).then_inc(xs_in[h], 16)

            load(0, 0)
            load(1, 1)
            with act.Fori(0, NX // 2) as i:
                for h in two:
                    for m in range(3):
                        high(i * 2 + h, m, i * 6 + (3 * h + m), (3 * h + m) % 2)
                        if m != 1:
                            q = (h * 2 + (m == 2))
                            load(i * 4 + q + 2, q % 2)
            with act.Fori(0, (NS - 19) // 2) as i:
                load(i * 2 + 18, 0)
                load(i * 2 + 19, 1)
            load(NS - 1, 0)

        @block.tensor
        def _(pe):
            pe.wait_ge(ready, 5)
            pe.wait_ge(ranks, 1)
            flat = oh[:, :, :].rearrange("p t e -> p (t e)")
            pe.matmul(k.psum[6][0:TR, 0:NT * NX], tri[:, :], flat, start=True, stop=True)
            pe.matmul(k.psum[7][:, 0:NT * NX], k.ones[0:TR, :], flat, start=True, stop=True).then_inc(ranks, 1)

            def turn(e, m, n, s):
                pe.wait_ge(raw_in[m], e * (32 if m < 2 else 16) + (32 if m < 2 else 16))
                pe.wait_ge(wt_lo, n + 1)
                if m < 2:
                    src = RAW[m][:, :].rearrange("p (j c) -> p j c", c=C)
                    for b in range(CB):
                        for j in range(4):
                            pe.transpose(PB[s][b][:, j * 128:(j + 1) * 128], src[:, j, b * 128:(b + 1) * 128], k.ident[:, :])
                        for j in range(4, HB):
                            last = pe.transpose(PB[s][2][:, b * C + (j - 4) * 128:b * C + (j - 3) * 128], src[:, j, b * 128:(b + 1) * 128], k.ident[:, :])
                else:
                    for j in range(HB):
                        for b in range(CB):
                            h0 = b * H + hidden_start(j)
                            last = pe.transpose(PB[s][j // 2][:, (j % 2) * C + b * 128:(j % 2) * C + (b + 1) * 128], RAW[m][:, h0:h0 + 128], k.ident[:, :])
                last.then_inc(wt_full, 1)

            experts(pe, turn)

        @block.vector
        def _(dve):
            tt, ts, red, drain = dve.tensor_tensor, dve.tensor_scalar, dve.tensor_reduce, dve.drain
            wide = lambda a: a.unsqueeze(2).to_broadcast(sh)
            dve.sem_inc(wt_full, 3)
            dve.sem_inc(wt_lo, 2)
            red(m1[:, :], k.LG[:, :, :], AX.X, ALU.max)
            drain()
            tt(prob[:, :, :], k.LG[:, :, :], wide(m1[:, :]), ALU.subtract).then_inc(shifted, 1)
            dve.wait_ge(exped, 1)
            red(den[:, :], prob[:, :, :], AX.X, ALU.add)
            drain()
            dve.reciprocal(den[:, :], den[:, :])
            drain()
            tt(prob[:, :, :], prob[:, :, :], wide(den[:, :]), ALU.mult)
            drain()
            dve.wait_ge(ready, 5)
            for m, f, w, o in ((m1, f1, w1, oh1), (m2, f2, w2, oh2)):
                red(m[:, :], prob[:, :, :], AX.X, ALU.max)
                drain()
                tt(w[:, :, :], prob[:, :, :], wide(m[:, :]), ALU.is_equal)
                drain()
                tt(w[:, :, :], w[:, :, :], back[:, :].unsqueeze(1).to_broadcast(sh), ALU.mult)
                drain()
                red(f[:, :], w[:, :, :], AX.X, ALU.max)
                drain()
                tt(o[:, :, :], w[:, :, :], wide(f[:, :]), ALU.is_equal)
                drain()
                if o is oh1:
                    dve.scalar_tensor_tensor(prob[:, :, :], o[:, :, :], -2.0, prob[:, :, :], ALU.mult, ALU.add)
                    drain()
            tt(oh[:, :, :], oh1[:, :, :], oh2[:, :, :], ALU.add)
            drain()
            dve.sem_inc(ranks, 1)
            tt(den[:, :], m1[:, :], m2[:, :], ALU.add)
            drain()
            ts(den[:, :], den[:, :], 1e-9, None, ALU.add)
            drain()
            dve.reciprocal(den[:, :], den[:, :])
            drain()
            for i, m in enumerate((m1, m2)):
                dve.scalar_tensor_tensor(extra[:, :, i], m[:, :], 1.0 / (SG * SW), den[:, :], ALU.mult, ALU.mult)
            ts(extra[:, :, 2], f1[:, :], -1.0, float(NX), ALU.mult, ALU.add)
            dve.tensor_copy(extra[:, :, 3].bitcast(I32), ids[:, :])
            drain()
            dve.sem_inc(extra_done, 1)
            dve.wait_ge(ranks, 2)
            tot = k.psum[7][:, 0:NT * NX].rearrange("p (t e) -> p t e", e=NX)
            dve.tensor_copy(run[0][:, :, :], tot)
            drain()
            step, cur = 1, 0
            while step < NT:
                a, b = run[cur], run[1 - cur]
                tt(b[:, step:NT, :], a[:, step:NT, :], a[:, 0:NT - step, :], ALU.add)
                dve.tensor_copy(b[:, 0:step, :], a[:, 0:step, :])
                drain()
                step, cur = step * 2, 1 - cur
            acc = run[cur]
            ts(tiles[:, :], acc[:, NT - 1, :], 127.0, None, ALU.add)
            drain()
            dve.tensor_copy(tilesi[:, :], tiles[:, :])
            drain()
            ts(tilesi[:, :], tilesi[:, :], 7, None, ALU.arith_shift_right)
            drain()
            dve.tensor_copy(tiles[:, :], tilesi[:, :])
            drain()
            dve.tensor_copy(cnt[0][:, :], tiles[:, :])
            drain()
            step, c = 1, 0
            while step < NX:
                a, b = cnt[c], cnt[1 - c]
                tt(b[:, step:NX], a[:, step:NX], a[:, 0:NX - step], ALU.add)
                dve.tensor_copy(b[:, 0:step], a[:, 0:step])
                drain()
                step, c = step * 2, 1 - c
            ends = cnt[c]
            tt(base[:, :], ends[:, :], tiles[:, :], ALU.subtract)
            drain()
            ts(base[:, :], base[:, :], 128.0, None, ALU.mult)
            tt(acc[:, :, :], acc[:, :, :], tot, ALU.subtract)
            drain()
            tt(acc[0:TR, :, :], acc[0:TR, :, :], k.psum[6][0:TR, 0:NT * NX].rearrange("p (t e) -> p t e", e=NX), ALU.add)
            drain()
            tt(acc[0:TR, :, :], acc[0:TR, :, :], base[0:TR, :].unsqueeze(1).to_broadcast(sh), ALU.add)
            drain()
            for i, (o, w) in enumerate(((oh1, w1), (oh2, w2))):
                tt(w[:, :, :], o[:, :, :], acc[0:TR, :, :], ALU.mult)
                drain()
                red(posf[:, :, i], w[:, :, :], AX.X, ALU.add)
            drain()
            dve.tensor_copy(pos[:, :, :], posf[:, :, :])
            tt(iot[:, :, :], iof[:, :].unsqueeze(2).to_broadcast([128, FT + 1, NX]),
               ends[:, :].unsqueeze(1).to_broadcast([128, FT + 1, NX]), ALU.is_ge)
            drain()
            red(tef[:, :], iot[:, :, :], AX.X, ALU.add)
            drain()
            ts(tef[:, :], tef[:, :], float(NX - 1), None, ALU.min)
            drain()
            dve.tensor_copy(te[:, :], tef[0:1, :])
            drain()
            dve.sem_inc(routed, 1)

            def low(e, m, n, s):
                dve.wait_ge(wt_hi, n + 1)
                for (bank, cols, to, masked), (_, _, hi, _) in zip(pieces(m, e, 1), pieces(m, e, 0)):
                    last = dve.scalar_tensor_tensor(to, cols(PB[s][bank]), k.hmask[:, :] if masked else SW, hi, ALU.mult, ALU.subtract)
                last.then_inc(wt_lo, 1)

            experts(dve, low)


def expert_stage(k, st, W, te, tef):
    nc, sb, sem = k.nc, k.sb, k.sem
    two = range(2)
    HH = HB // 2
    XG = [sb(f"rows{h}", [128, ROW], F32, st) for h in two]
    X16 = [sb(f"rowsT_parts{h}", [128, 2, CB, 128], F16, st) for h in two]
    SIL = [sb(f"silu{s}", [128, HH * 128], F32, st) for s in two]
    GF = [sb(f"gated{s}", [128, HH * 128], F32, st) for s in two]
    G16 = [sb(f"gated_parts{h}", [128, 2, HB * 128], F16, st) for h in two]
    YS = [sb(f"expert_out{h}", [128, C], F32, st) for h in two]
    IDS = [sb(f"token_index{h}", [128, 1], I32, st) for h in two]
    gate = sb("row_gates", [128, FT + 1], F32, st)
    token = sb("row_tokens", [128, FT + 1], I32, st)
    gd = sb("gate_terms", [128, 2], F32, st)
    xg_in = [sem(f"rows_in{h}") for h in two]
    xt_full, x_hi, x_done = sem("rowsT_full"), sem("rowsT_high"), sem("rowsT_done")
    h_full, silu_done, g_done, g_hi, g_lo = (sem(n) for n in ("hidden_half_full", "silu_done", "gated_done", "gated_high", "gated_low"))
    y_full, y_done, y_index, added, landed, out_done, pe_turn, act_turn = (sem(n) for n in (
        "expert_psum_full", "expert_out_done", "expert_index_done", "rows_added", "rows_landed", "out_written", "pe_turn", "act_turn"))
    H1, H3, XP, YP = k.psum[0:2], k.psum[2:4], k.psum[4], k.psum[5:7]

    def tiles(eng, body):
        body(0, 0, False, False)
        body(1, 1, False, True)
        with eng.Fori(1, FT // 2) as i:
            for h in two:
                body(i * 2 + h, h, True, True)

    def w(e, part, lo, n):
        return W[:, bass.ds(e, 1), part:part + 1, lo:lo + n].rearrange("q a b n -> q (a b n)")

    with nc.Block() as block:
        @block.sync
        def _(sp):
            def load(i, h):
                sp.wait_ge(x_done, i + 1)
                sp.dma_start(XG[h][:, :], k.disp_d[bass.ds(i * 128, 128), :]).then_inc(xg_in[h], 16)

            pairs(sp, FT + 1, load)
            sp.wait_ge(added, 16 * FT)
            sp.dma_start(k.out.rearrange("(a n) c -> a (n c)", a=TR), k.acc_d[0:N, :].rearrange("(a n) c -> a (n c)", a=TR)).then_inc(out_done, 16)
            sp.wait_ge(out_done, 16)

        @block.gpsimd
        def _(pool):
            def add(i, h):
                pool.wait_ge(y_done, i + 3)
                pool.wait_ge(y_index, i + 1)
                if not (isinstance(i, int) and i == 0):
                    pool.wait_ge(added, i * 16)
                pool.sem_inc(landed, 1)
                pool.indirect_dma_start(out=k.acc_d[:, :], out_offset=bass.IndirectOffsetOnAxis(ap=IDS[h][:, 0:1], axis=0),
                                        in_=YS[h][:, :], in_offset=None, compute_op=ALU.add).then_inc(added, 16)

            pairs(pool, FT, add)

        @block.tensor
        def _(pe):
            def turn(i, h):
                pe.wait_ge(xg_in[h], (i - h) * 8 + 16)
                pe.wait_ge(x_done, i + 2)
                for b in range(CB):
                    last = pe.transpose(XP[:, b * 128:(b + 1) * 128], XG[h][:, b * 128:(b + 1) * 128], k.ident[:, :])
                last.then_inc(xt_full, 1)

            def hidden(i, h, s, e):
                pe.wait_ge(x_done, i + 3)
                pe.wait_ge(g_done, i * 2 + s + 1)
                pe.sem_inc(pe_turn, 1)
                for m, bank in ((0, H1[s]), (1, H3[s])):
                    for jj in range(HH):
                        h0 = hidden_start(HH * s + jj)
                        n = 0
                        for b in range(CB):
                            for wp, xp in ((0, 0), (0, 1), (1, 0)):
                                last = pe.matmul(bank[:, jj * 128:(jj + 1) * 128], w(e, wp, m * CB * H + b * H + h0, 128),
                                                 X16[h][:, xp, b, :], start=n == 0, stop=n == 3 * CB - 1)
                                n += 1
                last.then_inc(h_full, 1)

            def down(i, h, e):
                pe.wait_ge(g_lo, i * 2 + 2)
                pe.wait_ge(y_done, i + 1)
                n = 0
                for j in range(HB):
                    for gp, wp in ((0, 0), (0, 1), (1, 0)):
                        last = pe.matmul(YP[h][:, 0:C], G16[h][:, gp, j * 128:(j + 1) * 128], w(e, wp, 2 * CB * H + j * C, C),
                                         start=n == 0, stop=n == 3 * HB - 1)
                        n += 1
                last.then_inc(y_full, 1)

            expert_of = lambda i: pe.value_load(te[0:1, bass.ds(i, 1)], min_val=0, max_val=NX - 1)
            turn(0, 0)

            def tile(i, h, _, before):
                e = expert_of(i)
                hidden(i, h, 0, e)
                turn(i + 1, 1 - h)
                hidden(i, h, 1, e)
                if before:
                    down(i - 1, 1 - h, expert_of(i - 1))

            tiles(pe, tile)
            down(FT - 1, (FT - 1) % 2, expert_of(FT - 1))

        @block.scalar
        def _(act):
            def rows_high(i, h):
                act.wait_ge(xt_full, i + 1)
                act.activation(X16[h][:, 0, :, :], XP[:, 0:C].rearrange("p (b n) -> p b n", b=CB), ACT.Copy, scale=SX).then_inc(x_hi, 1)

            def half(i, h, s):
                act.wait_ge(h_full, i * 2 + s + 1)
                act.activation(SIL[s][:, :], H1[s][:, 0:HH * 128], ACT.Silu, scale=1.0 / (SX * SW)).then_inc(silu_done, 1)
                act.wait_ge(g_done, i * 2 + s + 3)
                act.activation(G16[h][:, 0, s * HH * 128:(s + 1) * HH * 128], GF[s][:, :], ACT.Copy).then_inc(g_hi, 1)

            def out(i, h):
                act.wait_ge(y_full, i + 1)
                act.wait_ge(landed, i + 1)
                act.sem_inc(act_turn, 1)
                act.activation(YS[h][:, :], YP[h][:, 0:C], ACT.Copy, scale=gate[:, bass.ds(i, 1)])
                act.drain()
                act.sem_inc(y_done, 1)

            rows_high(0, 0)

            def tile(i, h, before2, before):
                half(i, h, 0)
                rows_high(i + 1, 1 - h)
                if before2:
                    out(i - 2, h)
                half(i, h, 1)

            tiles(act, tile)
            out(FT - 2, 0)
            out(FT - 1, 1)

        @block.vector
        def _(dve):
            dve.sem_inc(x_done, 2)
            dve.sem_inc(g_done, 2)
            dve.sem_inc(y_done, 2)
            dve.sem_inc(landed, 1)

            def rows_low(i, h):
                dve.wait_ge(x_hi, i + 1)
                dve.wait_ge(xg_in[h], (i - h) * 8 + 16)
                dve.scalar_tensor_tensor(X16[h][:, 1, :, :], XP[:, 0:C].rearrange("p (b n) -> p b n", b=CB), SX,
                                         X16[h][:, 0, :, :], ALU.mult, ALU.subtract)
                dve.tensor_tensor(gd[:, 0:1], XG[h][:, C:C + 1], XG[h][:, C + 1:C + 2], ALU.subtract)
                dve.tensor_scalar(gd[:, 1:2], XG[h][:, C + 2:C + 3], tef[:, bass.ds(i, 1)], None, ALU.is_equal)
                dve.tensor_copy(token[:, bass.ds(i, 1)], XG[h][:, C + 3:C + 4].bitcast(I32))
                dve.drain()
                dve.scalar_tensor_tensor(gate[:, bass.ds(i, 1)], gd[:, 0:1], gd[:, 1:2], XG[h][:, C + 1:C + 2], ALU.mult, ALU.add)
                dve.drain()
                dve.sem_inc(x_done, 1)

            def half(i, h, s):
                dve.wait_ge(silu_done, i * 2 + s + 1)
                dve.scalar_tensor_tensor(GF[s][:, :], H3[s][:, 0:HH * 128], SG / (SX * SW), SIL[s][:, :], ALU.mult, ALU.mult).then_inc(g_done, 1)
                dve.wait_ge(g_hi, i * 2 + s + 1)
                cols = slice(s * HH * 128, (s + 1) * HH * 128)
                dve.tensor_tensor(G16[h][:, 1, cols], GF[s][:, :], G16[h][:, 0, cols], ALU.subtract).then_inc(g_lo, 1)

            def index(i, h):
                dve.wait_ge(landed, i + 1)
                dve.tensor_copy(IDS[h][:, :], token[:, bass.ds(i, 1)]).then_inc(y_index, 1)

            rows_low(0, 0)

            def tile(i, h, before2, before):
                half(i, h, 0)
                rows_low(i + 1, 1 - h)
                if before2:
                    index(i - 2, h)
                half(i, h, 1)

            tiles(dve, tile)
            index(FT - 2, 0)
            index(FT - 1, 1)


_INS = ['x', 'src', 'dst', 'edge_attr_256', 'L0_gnn_W1', 'L0_gnn_b1', 'L0_gnn_bn_gamma', 'L0_gnn_bn_beta', 'L0_gnn_W2',
        'L0_gnn_b2', 'L0_gnn_ln_w', 'L0_gnn_ln_b', 'L0_gnn_gn_w', 'L0_gnn_gn_b', 'L0_gnn_gn_ms', 'L0_mix_W_qkv',
        'L0_mix_b_qkv', 'L0_mix_W_out', 'L0_mix_b_out', 'L0_ffn_router_w', 'L0_ffn_w1', 'L0_ffn_w2', 'L0_ffn_w3']


def kernel(**inputs):
    import numpy as np
    import concourse.bacc as bacc
    from concourse.bass_utils import run_bass_kernel_spmd

    nc = bacc.Bacc("TRN2", target_bir_lowering=False, num_devices=1)
    arrays, aps = {}, {}
    for name in _INS:
        a = np.ascontiguousarray(inputs[name])
        arrays[f"in_{name}"] = a
        aps[name] = nc.dram_tensor(f"in_{name}", a.shape, mybir.dt.from_np(a.dtype), kind="ExternalInput").ap()
    out = nc.dram_tensor("out", (N, C), F32, kind="ExternalOutput").ap()
    build(nc, aps, out)
    r = run_bass_kernel_spmd(nc, [arrays], core_ids=[0])
    return r.results[0]["out"]
```

```python
import math
from contextlib import ExitStack

import concourse.bass as bass
from concourse import mybir

F32 = mybir.dt.float32
F16 = mybir.dt.float16
I32 = mybir.dt.int32
ALU = mybir.AluOpType
ACT = mybir.ActivationFunctionType
AX = mybir.AxisListType

N = 6250
C = 256
E = 106250
CB = C // 128
TR = 125
NT = N // TR
HID = 2 * C
FB = HID // 128
CH = 250
NC = N // CH
EB = 1024
EK = EB // 128
NB = -(-E // EB)
LAST = E - EB
SEEN = (NB - 1) * EB - LAST
WIN = 128
NX = 8
H = 682
HB = -(-H // 128)
HM = 128 * (HB - 1)
TAIL = H - HM
TAIL3 = 64
T3 = slice(TAIL3, TAIL3 + TAIL)
PAIRS = 2 * N
TAILS = 2 * CB * HM
W2S = TAILS + CB * 128
WL = W2S + HB * C
TT = 256
FT = (PAIRS + NX * (TT - 1)) // TT
USUAL = FT - 2
ROW = C + 4
EPS = 1e-5
EPS_DIV = 1e-7
EPS_NORM = 1e-12
SX, SW, SG = 64.0, 256.0, 16.0


SPLIT = TR // 16 * 16
MOVED = 32


def move_rows(eng, out, in_, sem):
    for part in (slice(0, SPLIT), slice(SPLIT, TR)):
        eng.dma_start(out[part], in_[part]).then_inc(sem, 16)


def moved(n, h):
    return (n - h) * (MOVED // 2)


class K:
    pass


def pairs(eng, n, body):
    for h in range(2):
        body(h, h)
    if n // 2 > 1:
        with eng.Fori(1, n // 2) as i:
            for h in range(2):
                body(i * 2 + h, h)
    if n % 2:
        body(n - 1, (n - 1) % 2)


def first_two(n):
    return isinstance(n, int) and n < 2


def the_first(n):
    return isinstance(n, int) and n == 0


def build(nc, A, out):
    k = K()
    with ExitStack() as ctx:
        k.nc, k.A, k.out = nc, A, out
        k.sem = lambda name: ctx.enter_context(nc.semaphore(name))
        k.psum = [ctx.enter_context(nc.psum_tensor(f"bank{i}", [128, 512], F32)) for i in range(8)]

        def sb(name, shape, dt=F32, where=ctx):
            return where.enter_context(nc.sbuf_tensor(name, shape, dt))

        k.sb = sb
        k.xn_d = nc.dram_tensor("xn_rows", (N, C), F32, kind="Internal").ap()
        k.tok_d = nc.dram_tensor("token_rows", (N, ROW), F32, kind="Internal").ap()
        k.r_d = nc.dram_tensor("residual_rows", (N, C), F32, kind="Internal").ap()
        k.acc_d = nc.dram_tensor("output_rows", (N + TT, C), F32, kind="Internal").ap()
        k.disp_d = nc.dram_tensor("dispatched_rows", ((FT + 1) * TT, ROW), F32, kind="Internal").ap()
        k.ident = sb("ident", [128, 128])
        k.ones = sb("ones", [128, 128])
        k.rwT = sb("router_wT", [128, CB, NX])
        k.hmask = sb("hidden_mask", [128, 1])
        k.consts = k.sem("consts_ready")
        k.eps = sb("eps", [128, 1])
        k.pool_turn = k.sem("pool_turn")
        k.CONST = 6
        k.LG = sb("logits", [TR, NT, NX])
        k.gsc = sb("norm_scale", [128, CB])
        k.gbi = sb("norm_bias", [128, CB])
        with ExitStack() as big:
            k.UT = sb("node_sumT", [128, CB, N + WIN], F32, big)
            with ExitStack() as mid:
                k.XNT = sb("xnT", [128, CB, N], F32, mid)
                with ExitStack() as low:
                    tables(k, low)
                    with ExitStack() as st:
                        layernorm_stage(k, st)
                    with ExitStack() as st:
                        edge_mix_stage(k, st)
                    with ExitStack() as st:
                        stray_stage(k, st)
            with ExitStack() as st:
                gnn_mlp_stage(k, st)
            with ExitStack() as st:
                residual_stage(k, st)
        with ExitStack() as st:
            moe_stage(k, st)


def tables(k, st):
    k.src = k.sb("src_table", [128, NB + 2, EK], I32, st)
    k.dstl = k.sb("dst_in_window", [128, NB, EK], F32, st)
    k.basei = k.sb("window_base", [1, NB], I32, st)
    k.wqkv = k.sb("w_qkv", [128, CB, 3 * C], F32, st)
    k.wout = k.sb("w_out", [128, CB, C], F32, st)
    k.bq = k.sb("b_q", [128, CB], F32, st)
    k.bkv = k.sb("b_kv_rows", [128, 2 * C], F32, st)
    k.vwi = k.sb("w_v_out_plus_identity", [128, CB, C], F32, st)
    k.bb = k.sb("bias_rows", [128, C], F32, st)
    k.iota = k.sb("iota_window", [128, WIN], F32, st)
    k.GA = [k.sb(f"gathered{h}", [128, EK, C], F32, st) for h in range(2)]
    k.IDX = [k.sb(f"src_index{h}", [128, EK], I32, st) for h in range(2)]
    k.g_in = [k.sem(f"gathered_in{h}") for h in range(2)]
    k.strays = k.sb("stray_count", [1, 1], I32, st)


def layernorm_stage(k, st):
    nc, sb, sem, A = k.nc, k.sb, k.sem, k.A
    G = 10
    NG = NT // G
    ON_ACT = 3
    BANKS = 5
    X = [sb(f"x_in{h}", [TR, G, C], F32, st) for h in range(2)]
    XN = [sb(f"xn{h}", [TR, G, C], F32, st) for h in range(2)]
    stats = sb("ln_stats", [TR, G, 6], F32, st)
    mv = sb("ln_mv", [TR, G, 2], F32, st)
    rstd = sb("ln_rstd", [TR, G], F32, st)
    std = sb("ln_std", [TR, G], F32, st)
    nmr = sb("ln_minus_mean_rstd", [TR, G], F32, st)
    var_done, std_done, scale_done, xn_act = (sem(n) for n in ("ln_var_done", "ln_std_done", "ln_scale_done", "xn_done_scalar"))
    dsti = sb("dst_table", [128, NB, EK], I32, st)
    basef = sb("window_base_f", [1, NB], F32, st)
    bq_row = sb("b_qkv_rows", [128, 3 * C], F32, st)
    b_out_row = sb("b_out_rows", [128, C], F32, st)
    bv_col = sb("b_v", [128, CB], F32, st)
    bv_wide = sb("b_v_wide", [128, CB, 128], F32, st)
    wvT = sb("w_vT", [128, CB, C], F32, st)
    msum = sb("mean_sums", [128, 2, CB + 1], F32, st)
    rw = sb("router_w", [NX, C], F32, st)
    x_in = [sem(f"x_in_{h}") for h in range(2)]
    xn_done, x_free, xn_st = sem("xn_done"), sem("x_free"), [sem(f"xn_stored_{h}") for h in range(2)]
    tr_full, tr_free = sem("tr_full"), sem("tr_free")
    tab_in, seen_out, prep_v, prep_p, base_full = sem("tables_in"), sem("seen_masked"), sem("prep_vector"), sem("prep_tensor"), sem("base_full")
    idx_first = sem("first_index_ready")
    k.seen_out = seen_out
    TAB = 16 * 13
    bank = k.psum

    with nc.Block() as block:
        @block.sync
        def _(sp):
            def load(n, h):
                sp.wait_ge(x_free, n + 1)
                move_rows(sp, X[h][:, :, :], A["x"][bass.ds(n * (G * TR), G * TR), :].rearrange("(g p) c -> p g c", g=G), x_in[h])

            pairs(sp, NG, load)
            body = (NB - 1) * EB
            t = lambda name: A[name]
            sp.dma_start(dsti[:, 0:NB - 1, :], t("dst")[0:body].rearrange("(b p k) -> p b k", p=128, k=EK)).then_inc(tab_in, 16)
            sp.dma_start(dsti[:, NB - 1, :], t("dst")[LAST:E].rearrange("(p k) -> p k", k=EK)).then_inc(tab_in, 16)
            sp.dma_start(k.src[:, 0:NB - 1, :], t("src")[0:body].rearrange("(b p k) -> p b k", p=128, k=EK)).then_inc(tab_in, 16)
            sp.dma_start(k.src[:, NB - 1, :], t("src")[LAST:E].rearrange("(p k) -> p k", k=EK)).then_inc(tab_in, 16)
            with nc.allow_non_contiguous_dma("one word of each batch"):
                sp.dma_start(k.basei[0:1, 0:NB - 1], t("dst")[0:body].rearrange("(a b k) -> a b k", a=1, k=EB)[:, :, 0]).then_inc(tab_in, 16)
                sp.dma_start(k.basei[0:1, NB - 1:NB], t("dst")[LAST:LAST + 1].rearrange("(a b) -> a b", a=1)).then_inc(tab_in, 16)
                sp.dma_start(k.bq[:, :], t("L0_mix_b_qkv")[0:C].rearrange("(b p) -> p b", p=128)).then_inc(tab_in, 16)
                sp.dma_start(bv_col[:, :], t("L0_mix_b_qkv")[2 * C:3 * C].rearrange("(b p) -> p b", p=128)).then_inc(tab_in, 16)
            sp.dma_start(k.wqkv[:, :, :], t("L0_mix_W_qkv").rearrange("(b p) n -> p b n", p=128)).then_inc(tab_in, 16)
            sp.dma_start(k.wout[:, :, :], t("L0_mix_W_out").rearrange("(b p) n -> p b n", p=128)).then_inc(tab_in, 16)
            sp.dma_start(bq_row[:, :], t("L0_mix_b_qkv").partition_broadcast(128)).then_inc(tab_in, 16)
            sp.dma_start(b_out_row[:, :], t("L0_mix_b_out").partition_broadcast(128)).then_inc(tab_in, 16)
            sp.dma_start(rw[:, :], t("L0_ffn_router_w")).then_inc(tab_in, 16)

        @block.scalar
        def _(act):
            def copy_out(n, h):
                act.wait_ge(k.consts, k.CONST)
                act.wait_ge(var_done, n + 1)
                act.activation(std[:, :], mv[:, :, 1], ACT.Sqrt, bias=k.eps[0:TR, :]).then_inc(std_done, 1)
                act.wait_ge(k.consts, k.CONST)
                act.wait_ge(scale_done, n + 1)
                for g in range(G - ON_ACT, G):
                    last = act.activation(XN[h][:, g, :], X[h][:, g, :], ACT.Identity, scale=rstd[:, g:g + 1], bias=nmr[:, g:g + 1])
                last.then_inc(xn_act, 1)
                for g in range(G):
                    m = n * G + g
                    act.wait_ge(k.consts, k.CONST)
                    act.wait_ge(tr_full, m + 1)
                    p = bank[g % BANKS][:, 0:CB * TR].rearrange("p (b c) -> p b c", b=CB)
                    act.activation(k.XNT[:, :, bass.ds(m * TR, TR)], p, ACT.Copy)
                    act.activation(k.UT[:, :, bass.ds(m * TR, TR)], p, ACT.Copy).then_inc(tr_free, 1)

            pairs(act, NG, copy_out)

        @block.gpsimd
        def _(pool):
            pool.memset(k.ident[:, :], 0.0)
            pool.memset(k.ones[:, :], 1.0).then_inc(k.consts, 1)
            pool.memset(k.eps[:, :], EPS).then_inc(k.consts, 1)
            pool.memset(k.hmask[:, :], SW).then_inc(k.consts, 1)
            pool.iota(k.iota[:, :], [[1, WIN]], base=0, channel_multiplier=0,
                      allow_small_or_imprecise_dtypes=True).then_inc(k.consts, 1)
            pool.memset(k.src[:, NB:NB + 2, :], 0).then_inc(seen_out, 1)
            pool.memset(k.UT[:, :, N:N + WIN], 0.0).then_inc(seen_out, 1)
            pool.drain()
            pool.affine_select(out=k.ident[:, :], in_=k.ident[:, :], compare_op=ALU.not_equal, fill=1.0,
                               base=0, pattern=[[-1, 128]], channel_multiplier=1).then_inc(k.consts, 1)
            pool.affine_select(out=k.hmask[:, :], in_=k.hmask[:, :], compare_op=ALU.is_ge, fill=0.0,
                               base=-TAIL3, pattern=[[0, 1]], channel_multiplier=1).then_inc(k.consts, 1)

            def store(n, h):
                pool.wait_ge(k.consts, k.CONST)
                pool.wait_ge(xn_done, n + 1)
                pool.wait_ge(xn_act, n + 1)
                move_rows(pool, k.xn_d[bass.ds(n * (G * TR), G * TR), :].rearrange("(g p) c -> p g c", g=G), XN[h][:, :, :], xn_st[h])

            pairs(pool, NG, store)
            pool.wait_ge(tab_in, TAB)
            pool.tensor_copy(k.IDX[0][:, :], k.src[:, 0, :]).then_inc(idx_first, 1)
            for h in range(2):
                pool.wait_ge(xn_st[h], MOVED * ((NG + 1 - h) // 2))
            pool.wait_ge(idx_first, 1)
            for e in range(EK):
                pool.indirect_dma_start(out=k.GA[0][:, e, :], out_offset=None, in_=k.xn_d[:, :],
                                        in_offset=bass.IndirectOffsetOnAxis(ap=k.IDX[0][:, e:e + 1], axis=0)).then_inc(k.g_in[0], 16)
            pool.wait_ge(prep_v, 2)
            pool.affine_select(out=k.dstl[:, NB - 1, :], in_=k.dstl[:, NB - 1, :], compare_op=ALU.is_ge, fill=0.5,
                               base=-SEEN, pattern=[[1, EK]], channel_multiplier=EK).then_inc(seen_out, 1)

        @block.vector
        def _(dve):
            dve.sem_inc(x_free, 2)
            dve.sem_inc(tr_free, BANKS)

            def norm(n, h):
                dve.wait_ge(k.consts, k.CONST)
                dve.wait_ge(x_in[h], moved(n, h) + MOVED)
                for g in range(G):
                    dve.bn_stats(stats[:, g, :], X[h][:, g, :])
                dve.drain()
                for g in range(G):
                    dve.bn_aggr(mv[:, g, :], stats[:, g, :])
                dve.drain()
                dve.sem_inc(var_done, 1)
                dve.wait_ge(k.consts, k.CONST)
                dve.wait_ge(std_done, n + 1)
                dve.reciprocal(rstd[:, :], std[:, :])
                dve.drain()
                if not first_two(n):
                    dve.wait_ge(xn_st[h], moved(n, h))
                    dve.wait_ge(tr_free, n * G + BANKS - G)
                dve.scalar_tensor_tensor(nmr[:, :], mv[:, :, 0], -1.0, rstd[:, :], ALU.mult, ALU.mult).then_inc(scale_done, 1)
                for g in range(G - ON_ACT):
                    last = dve.tensor_scalar(XN[h][:, g, :], X[h][:, g, :], mv[:, g, 0:1], rstd[:, g:g + 1],
                                             ALU.subtract, ALU.mult)
                last.then_inc(xn_done, 1)
                dve.drain()
                dve.wait_ge(k.consts, k.CONST)
                dve.wait_ge(xn_act, n + 1)
                dve.sem_inc(x_free, 1)

            pairs(dve, NG, norm)
            dve.wait_ge(tab_in, TAB)
            dve.tensor_copy(basef[:, :], k.basei[:, :]).then_inc(prep_v, 1)
            for j in range(2):
                for b in range(CB):
                    dve.tensor_reduce(msum[:, j, b:b + 1], k.wqkv[:, b, j * C:(j + 1) * C], AX.X, ALU.add)
                dve.tensor_reduce(msum[:, j, CB:CB + 1], bq_row[:, j * C:(j + 1) * C], AX.X, ALU.add)
            for b in range(CB):
                dve.tensor_scalar(bv_wide[:, b, :], k.ones[:, :], bv_col[:, b:b + 1], None, ALU.mult)
            dve.drain()
            dve.tensor_scalar(msum[:, :, :], msum[:, :, :], 1.0 / C, None, ALU.mult)
            dve.drain()
            for j in range(2):
                for b in range(CB):
                    w = k.wqkv[:, b, j * C:(j + 1) * C]
                    dve.tensor_scalar(w, w, msum[:, j, b:b + 1], None, ALU.subtract)
            dve.tensor_scalar(k.bq[:, :], k.bq[:, :], msum[:, 0, CB:CB + 1], None, ALU.subtract)
            dve.tensor_scalar(k.bkv[:, 0:C], bq_row[:, C:2 * C], msum[:, 1, CB:CB + 1], None, ALU.subtract)
            dve.tensor_copy(k.bkv[:, C:2 * C], bq_row[:, 2 * C:3 * C])
            dve.wait_ge(base_full, 1)
            dve.tensor_copy(k.dstl[:, :, :], dsti[:, :, :])
            dve.drain()
            dve.tensor_tensor(k.dstl[:, :, :], k.dstl[:, :, :],
                              bank[5][:, 0:NB].unsqueeze(2).to_broadcast([128, NB, EK]), ALU.subtract).then_inc(prep_v, 1)
            dve.wait_ge(prep_p, 1)
            dve.tensor_copy(wvT[:, :, :], bank[6][:, :].rearrange("p (b c) -> p b c", b=CB)).then_inc(prep_v, 1)
            dve.tensor_copy(k.rwT[:, :, :], bank[7][:, 0:CB * NX].rearrange("p (b c) -> p b c", b=CB)).then_inc(prep_v, 1)
            dve.wait_ge(prep_p, 2)
            dve.tensor_copy(k.vwi[:, :, :], bank[6][:, :].rearrange("p (b c) -> p b c", b=CB))
            dve.tensor_tensor(k.bb[:, :], bank[7][:, 0:C], b_out_row[:, :], ALU.add)
            dve.drain()
            for b in range(CB):
                d = k.vwi[:, b, b * 128:(b + 1) * 128]
                dve.tensor_tensor(d, d, k.ident[:, :], ALU.add)


        @block.tensor
        def _(pe):
            pe.wait_ge(k.consts, k.CONST)

            def turn(n, h):
                pe.wait_ge(xn_done, n + 1)
                pe.wait_ge(xn_act, n + 1)
                for g in range(G):
                    pe.wait_ge(tr_free, n * G + g + 1)
                    for b in range(CB):
                        last = pe.transpose(bank[g % BANKS][:, b * TR:(b + 1) * TR], XN[h][:, g, b * 128:(b + 1) * 128],
                                            k.ident[0:TR, 0:TR])
                    last.then_inc(tr_full, 1)

            pairs(pe, NG, turn)
            pe.wait_ge(prep_v, 1)
            pe.matmul(bank[5][:, 0:NB], k.ones[0:1, :], basef[:, :], start=True, stop=True).then_inc(base_full, 1)
            pe.wait_ge(tab_in, TAB)
            for b in range(CB):
                for c in range(CB):
                    pe.transpose(bank[6][:, c * C + b * 128:c * C + (b + 1) * 128],
                                 k.wqkv[:, b, 2 * C + c * 128:2 * C + (c + 1) * 128], k.ident[:, :])
                last = pe.transpose(bank[7][:, b * NX:(b + 1) * NX], rw[:, b * 128:(b + 1) * 128], k.ident[0:NX, 0:NX])
            last.then_inc(prep_p, 1)
            pe.wait_ge(prep_v, 4)
            for b in range(CB):
                for c in range(CB):
                    pe.matmul(bank[6][:, b * C:(b + 1) * C], wvT[:, c, b * 128:(b + 1) * 128], k.wout[:, c, :],
                              start=c == 0, stop=c == CB - 1)
            for c in range(CB):
                last = pe.matmul(bank[7][:, 0:C], bv_wide[:, c, :], k.wout[:, c, :], start=c == 0, stop=c == CB - 1)
            last.then_inc(prep_p, 1)


def edge_mix_stage(k, st):
    nc, sb, sem, A = k.nc, k.sb, k.sem, k.A
    two = range(2)
    EA = [sb(f"edge_attr{h}", [128, EK, C], F32, st) for h in two]
    GA, IDX, g_in = k.GA, k.IDX, k.g_in
    MSG = [sb(f"message{h}", [128, EK, C], F32, st) for h in two]
    SEL = [sb(f"dst_select{h}", [128, EK, WIN], F32, st) for h in two]
    STG = [sb(f"xnT_tile{h}", [128, CB, TR], F32, st) for h in two]
    KV = [sb(f"key_value{h}", [TR, 2 * C], F32, st) for h in two]
    K2 = [sb(f"key_squared{h}", [TR, C], F32, st) for h in two]
    K4 = [sb(f"key_fourth{h}", [TR, C], F32, st) for h in two]
    VS = [sb(f"value_scaled{h}", [TR, C], F32, st) for h in two]
    KS = [sb(f"key_sum{h}", [TR, 1], F32, st) for h in two]
    RS = [sb(f"key_scale{h}", [TR, 1], F32, st) for h in two]
    Q2 = [sb(f"query_squared{h}", [128, CB, TR], F32, st) for h in two]
    Q4 = [sb(f"query_fourth{h}", [128, CB, TR], F32, st) for h in two]
    XT = [sb(f"x_tile{h}", [TR, C], F32, st) for h in two]
    RT = [sb(f"residual_tile{h}", [TR, C], F32, st) for h in two]
    KWX = sb("kv_out_weights", [128, CB, C + 1], F32, st)
    kvT = sb("kvT", [128, CB, C], F32, st)
    knorm = sb("key_norms", [128, CB], F32, st)
    qs = sb("query_scales", [TR, 4], F32, st)
    zero = sb("zero_row", [128, 2 * C], F32, st)
    PE_, KVP, KVT, NRM = k.psum[0:2], k.psum[2:4], k.psum[6], k.psum[7]
    QP, VP, TP = k.psum[2:4], k.psum[4:6], k.psum[6:8]
    gathers_begun = sem("gathers_begun")
    ea_in = [sem(f"edge_attr_in{h}") for h in two]
    stg_in = [sem(f"xnT_tile_in{h}") for h in two]
    xt_in = [sem(f"x_tile_in{h}") for h in two]
    r_out = [sem(f"residual_out{h}") for h in two]
    added, idx_ready, relu_done, sel_done = sem("edges_added"), sem("index_ready"), sem("relu_done"), sem("select_done")
    win_full, win_free = sem("window_full"), sem("window_free")
    kvp_full = sem("kv_psum_full")
    kv_done, ks_done, rs_done, k4_done, vs_done, kv_used = (sem(n) for n in (
        "key_value_done", "key_sum_done", "key_scale_done", "key_fourth_done", "value_scaled_done", "kv_used"))
    kvt_copied, kvt_scaled, norm_std, kw_full = sem("kvT_copied"), sem("kw_ready"), sem("key_norm_ready"), sem("kw_full")
    q_full, q_done, v_full, t_full, q_std, r_done, qs_sum, ready = (sem(n) for n in (
        "query_full", "query_done", "value_out_full", "mix_full", "query_norm_ready", "residual_done", "query_sums_done", "edge_stage_ready"))
    stray_in, stray_sum = sem("stray_counts_ready"), sem("strays_summed")
    stray_col = sb("stray_counts", [128, 1], F32, st)
    READY = 2

    def schedule(body):
        body(0, 1, 0, True)
        with body.eng.Fori(1, NT // 2) as i:
            body(i, 1, i * 2, False)
        body(NT // 2, None, None, False)
        body(NT // 2 + 1, 2, 0, True)
        body(NT // 2 + 2, 2, 2, False)
        with body.eng.Fori(NT // 2 + 3, NT + 1) as i:
            body(i, 2, i * 2 - (NT + 2), False)
        body(NT + 1, 3, None, False)

    def on(eng):
        def wrap(f):
            f.eng = eng
            schedule(f)
            return f
        return wrap

    def held(eng):
        eng.wait_ge(ready, READY)

    with nc.Block() as block:
        @block.sync
        def _(sp):
            @on(sp)
            def _(i, mix, t0, first):
                for h in two:
                    b = i * 2 + h
                    sp.wait_ge(added, b + 1)
                    lo = LAST if isinstance(b, int) and b == NB - 1 else b * EB
                    sp.dma_start(EA[h][:, :, :], A["edge_attr_256"][bass.ds(lo, EB), :]
                                 .rearrange("(p k) c -> p k c", k=EK)).then_inc(ea_in[h], 16)
                    if mix in (1, 2):
                        t = t0 + h
                        if mix == 2 and first:
                            sp.wait_ge(kvp_full, NT + 2)
                        sp.wait_ge(kvp_full if mix == 1 else v_full, t + 1)
                        sp.dma_start(STG[h][:, :, :], k.XNT[:, :, bass.ds(t * TR, TR)]).then_inc(stg_in[h], 16)
                    if mix == 2:
                        sp.wait_ge(r_done, t + 1)
                        move_rows(sp, XT[h][:, :], A["x"][bass.ds(t * TR, TR), :], xt_in[h])
                        if not first:
                            move_rows(sp, k.r_d[bass.ds(t * TR - 2 * TR, TR), :], RT[h][:, :], r_out[h])
                    if mix == 3:
                        t = NT - 2 + h
                        sp.wait_ge(r_done, t + 3)
                        move_rows(sp, k.r_d[bass.ds(t * TR, TR), :], RT[h][:, :], r_out[h])
            for h in two:
                sp.wait_ge(r_out[h], MOVED * (NT // 2))

        @block.gpsimd
        def _(pool):
            @on(pool)
            def _(i, mix, t0, first):
                for h in two:
                    b = i * 2 + h
                    if the_first(b):
                        continue
                    pool.wait_ge(idx_ready, b)
                    pool.wait_ge(added, b + 1)
                    pool.sem_inc(gathers_begun, 1)
                    for e in range(EK):
                        pool.indirect_dma_start(
                            out=GA[h][:, e, :], out_offset=None, in_=k.xn_d[:, :],
                            in_offset=bass.IndirectOffsetOnAxis(ap=IDX[h][:, e:e + 1], axis=0)).then_inc(g_in[h], 16)

        @block.vector
        def _(dve):
            dve.memset(zero[:, :], 0.0).then_inc(ready, 1)
            dve.memset(KWX[:, :, C:C + 1], 1.0).then_inc(ready, 1)
            for s, n in ((added, 2), (win_free, 2), (kvp_full, 2), (v_full, 2), (kv_done, 2), (kv_used, 2), (r_done, 2)):
                dve.sem_inc(s, n)
            dve.tensor_copy(IDX[1][:, :], k.src[:, 1, :]).then_inc(idx_ready, 1)

            low, high = (MSG[0][:, h * 4:h * 4 + 4, :].rearrange("p k c -> p (k c)")[:, 0:NB * EK] for h in two)
            every = k.dstl[:, :, :].rearrange("p b k -> p (b k)")
            dve.tensor_scalar(low, every, 0.0, None, ALU.is_lt)
            dve.tensor_scalar(high, every, float(WIN - 1), None, ALU.is_gt)
            dve.drain()
            dve.tensor_tensor(low, low, high, ALU.add)
            dve.drain()
            dve.tensor_reduce(stray_col[:, :], low, AX.X, ALU.add).then_inc(stray_in, 1)
            dve.drain()

            def to_window(b, h):
                dve.wait_ge(win_full, b + 1)
                dve.wait_ge(win_free, b + 2)
                base = dve.value_load(k.basei[0:1, bass.ds(b, 1)], min_val=0, max_val=N - 1)
                w = k.UT[:, :, bass.ds(base, WIN)]
                dve.tensor_tensor(w, w, PE_[h][:, 0:CB * WIN].rearrange("p (b n) -> p b n", b=CB), ALU.add)\
                    .then_inc(win_free, 1)

            def kv_scale(t, h):
                dve.wait_ge(ks_done, t + 1)
                dve.wait_ge(kv_used, t + 1)
                dve.tensor_scalar(RS[h][:, :], KS[h][:, :], EPS_DIV, None, ALU.add)
                dve.drain()
                dve.reciprocal(RS[h][:, :], RS[h][:, :]).then_inc(rs_done, 1)
                dve.drain()
                dve.tensor_scalar(VS[h][:, :], KV[h][:, C:2 * C], RS[h][:, :], None, ALU.mult).then_inc(vs_done, 1)

            def mix_sums(t, h):
                dve.wait_ge(t_full, t + 1)
                dve.tensor_scalar(qs[:, 0:2], TP[h][0:TR, C:C + 2], 0.0, None, ALU.add).then_inc(qs_sum, 1)
                dve.drain()

            def mix_out(t, h):
                dve.tensor_scalar(qs[:, 2:3], qs[:, 0:1], EPS_DIV, None, ALU.add)
                dve.drain()
                dve.reciprocal(qs[:, 2:3], qs[:, 2:3])
                dve.drain()
                dve.wait_ge(q_std, t + 1)
                dve.tensor_scalar(qs[:, 3:4], qs[:, 3:4], qs[:, 2:3], EPS_NORM, ALU.mult, ALU.max)
                dve.drain()
                dve.reciprocal(qs[:, 3:4], qs[:, 3:4])
                dve.drain()
                dve.tensor_scalar(qs[:, 2:3], qs[:, 2:3], qs[:, 3:4], 1.0 / math.sqrt(N), ALU.mult, ALU.mult)
                dve.drain()
                if not first_two(t):
                    dve.wait_ge(r_out[h], moved(t, h))
                dve.wait_ge(xt_in[h], moved(t, h) + MOVED)
                dve.scalar_tensor_tensor(RT[h][:, :], TP[h][0:TR, 0:C], qs[:, 2:3], XT[h][:, :], ALU.mult, ALU.add)
                dve.drain()
                dve.tensor_tensor(RT[h][:, :], RT[h][:, :], VP[h][0:TR, 0:C], ALU.add)
                dve.drain()
                dve.tensor_tensor(RT[h][:, :], RT[h][:, :], k.bb[0:TR, :], ALU.add).then_inc(r_done, 1)
                dve.drain()

            @on(dve)
            def _(i, mix, t0, first):
                for h in two:
                    b = i * 2 + h
                    dve.wait_ge(ea_in[h], i * 16 + 16)
                    dve.wait_ge(g_in[h], i * (16 * EK) + 16 * EK)
                    if not first_two(b):
                        dve.wait_ge(win_full, b - 1)
                    dve.tensor_tensor(MSG[h][:, :, :], GA[h][:, :, :], EA[h][:, :, :], ALU.add).then_inc(added, 1)
                    dve.tensor_copy(IDX[h][:, :], k.src[:, bass.ds(b + 2, 1), :].rearrange("p a k -> p (a k)")).then_inc(idx_ready, 1)
                    for e in range(EK):
                        last = dve.tensor_scalar(SEL[h][:, e, :], k.iota[:, :],
                                                 k.dstl[:, bass.ds(b, 1), e:e + 1].rearrange("p a k -> p (a k)"), None, ALU.is_equal)
                    last.then_inc(sel_done, 1)
                    if not the_first(b):
                        to_window(b - 1, 1 - h)
                    if mix == 1:
                        t = t0 + h
                        dve.wait_ge(kvp_full, t + 3)
                        dve.wait_ge(kv_used, t + 1)
                        dve.tensor_tensor(KV[h][:, :], KVP[h][0:TR, :], k.bkv[0:TR, :], ALU.add).then_inc(kv_done, 1)
                        kv_scale(t, h)
                    if mix is None and h == 0:
                        dve.wait_ge(kv_used, NT + 2)
                        dve.tensor_copy(kvT[:, :, :], KVT[:, :].rearrange("p (b c) -> p b c", b=CB)).then_inc(kvt_copied, 1)
                        dve.wait_ge(stray_sum, 1)
                        dve.tensor_copy(k.strays[:, :], VP[0][0:1, 0:1])
                        dve.wait_ge(norm_std, 1)
                        dve.tensor_scalar(knorm[:, :], knorm[:, :], EPS_NORM, None, ALU.max)
                        dve.drain()
                        dve.reciprocal(knorm[:, :], knorm[:, :])
                        dve.drain()
                        dve.wait_ge(kw_full, 1)
                        for c in range(CB):
                            last = dve.tensor_scalar(KWX[:, c, 0:C], KVT[:, c * C:(c + 1) * C], knorm[:, c:c + 1], None, ALU.mult)
                        last.then_inc(kvt_scaled, 1)
                    if mix == 2 and not (first and h == 0):
                        mix_sums(t0 + h - 1, 1 - h)
                        mix_out(t0 + h - 1, 1 - h)
                    if mix == 3 and h == 0:
                        mix_sums(NT - 1, 1)
                        mix_out(NT - 1, 1)
            to_window(NB - 1, 1)

        @block.scalar
        def _(act):
            @on(act)
            def _(i, mix, t0, first):
                for h in two:
                    b = i * 2 + h
                    act.wait_ge(added, b + 3)
                    act.activation(MSG[h][:, :, :], MSG[h][:, :, :], ACT.Relu).then_inc(relu_done, 1)
                    if mix == 1:
                        t = t0 + h
                        act.wait_ge(kv_done, t + 3)
                        act.activation(K2[h][:, :], KV[h][:, 0:C], ACT.Square, accum_out=KS[h][:, :]).then_inc(ks_done, 1)
                        act.drain()
                        act.wait_ge(rs_done, t + 1)
                        act.activation(K4[h][:, :], K2[h][:, :], ACT.Square, scale=RS[h][:, :]).then_inc(k4_done, 1)
                    if mix is None and h == 0:
                        act.wait_ge(kv_used, NT + 2)
                        act.activation(knorm[:, :], NRM[:, 0:CB], ACT.Sqrt).then_inc(norm_std, 1)
                    if mix == 2:
                        t = t0 + h
                        if not (first and h == 0):
                            act.wait_ge(qs_sum, t)
                            act.activation(qs[:, 3:4], qs[:, 1:2], ACT.Sqrt).then_inc(q_std, 1)
                        act.drain()
                        act.wait_ge(q_full, t + 1)
                        for c in range(CB):
                            act.activation(Q2[h][:, c, :], QP[h][:, c * TR:(c + 1) * TR], ACT.Square, bias=k.bq[:, c:c + 1])
                        act.drain()
                        act.activation(Q4[h][:, :, :], Q2[h][:, :, :], ACT.Square).then_inc(q_done, 1)
                    if mix == 3 and h == 0:
                        act.wait_ge(qs_sum, NT)
                        act.activation(qs[:, 3:4], qs[:, 1:2], ACT.Sqrt).then_inc(q_std, 1)

        @block.tensor
        def _(pe):
            held(pe)
            pe.matmul(KVT[:, :], zero[:, 0:128], zero[:, :], start=True, stop=False, skip_group_check=True)
            pe.matmul(NRM[:, 0:CB], zero[:, 0:128], zero[:, 0:CB], start=True, stop=False, skip_group_check=True)
            pe.wait_ge(stray_in, 1)
            pe.matmul(VP[0][0:1, 0:1], stray_col[:, :], k.ones[:, 0:1], start=True, stop=True).then_inc(stray_sum, 1)

            def kv_sums(t, h, done=False):
                held(pe)
                pe.wait_ge(k4_done, t + 1)
                pe.wait_ge(vs_done, t + 1)
                for c in range(CB):
                    pe.matmul(KVT[:, c * C:(c + 1) * C], VS[h][:, c * 128:(c + 1) * 128], K2[h][:, :],
                              start=False, stop=done, skip_group_check=True)
                for c in range(CB):
                    last = pe.matmul(NRM[:, c:c + 1], K4[h][:, c * 128:(c + 1) * 128], k.ones[0:TR, 0:1],
                                     start=False, stop=done, skip_group_check=True)
                last.then_inc(kv_used, 1)

            def mixed(t, h):
                held(pe)
                pe.wait_ge(q_done, t + 1)
                pe.wait_ge(r_done, t + 1)
                for c in range(CB):
                    pe.matmul(TP[h][0:TR, 0:C + 1], Q2[h][:, c, :], KWX[:, c, :], start=c == 0, stop=c == CB - 1)
                for c in range(CB):
                    last = pe.matmul(TP[h][0:TR, C + 1:C + 2], Q4[h][:, c, :], k.ones[:, 0:1], start=c == 0, stop=c == CB - 1)
                last.then_inc(t_full, 1)

            @on(pe)
            def _(i, mix, t0, first):
                for h in two:
                    b = i * 2 + h
                    if mix == 1 and not (first and h == 0):
                        kv_sums(t0 + h - 1, 1 - h)
                    if mix is None and h == 0:
                        kv_sums(NT - 1, 1, True)
                        pe.wait_ge(kvt_copied, 1)
                        pe.wait_ge(norm_std, 1)
                        for q in range(CB):
                            for c in range(CB):
                                last = pe.matmul(KVT[:, q * C:(q + 1) * C], kvT[:, c, q * 128:(q + 1) * 128], k.wout[:, c, :],
                                                 start=c == 0, stop=c == CB - 1)
                        last.then_inc(kw_full, 1)
                        pe.wait_ge(kvt_scaled, 1)
                    if mix == 2 and not (first and h == 0):
                        mixed(t0 + h - 1, 1 - h)
                    if mix == 3 and h == 0:
                        mixed(NT - 1, 1)
                    if mix in (1, 2):
                        t = t0 + h
                        pe.wait_ge(stg_in[h], ((t - h) * 8 + 16) + (mix - 1) * (8 * NT))
                    if mix == 1:
                        held(pe)
                        pe.wait_ge(kv_done, t + 1)
                        for c in range(CB):
                            last = pe.matmul(KVP[h][0:TR, :], STG[h][:, c, :], k.wqkv[:, c, C:3 * C], start=c == 0, stop=c == CB - 1)
                        last.then_inc(kvp_full, 1)
                    if mix == 2:
                        held(pe)
                        pe.wait_ge(r_done, t + 1)
                        if not (first):
                            pe.wait_ge(q_done, t - 1)
                        for q in range(CB):
                            for c in range(CB):
                                last = pe.matmul(QP[h][:, q * TR:(q + 1) * TR], k.wqkv[:, c, q * 128:(q + 1) * 128], STG[h][:, c, :],
                                                 start=c == 0, stop=c == CB - 1)
                        last.then_inc(q_full, 1)
                        for c in range(CB):
                            last = pe.matmul(VP[h][0:TR, 0:C], STG[h][:, c, :], k.vwi[:, c, :], start=c == 0, stop=c == CB - 1)
                        last.then_inc(v_full, 1)
                    held(pe)
                    pe.wait_ge(relu_done, b + 1)
                    pe.wait_ge(sel_done, b + 1)
                    pe.wait_ge(win_free, b + 1)
                    for c in range(CB):
                        for e in range(EK):
                            last = pe.matmul(PE_[h][:, c * WIN:(c + 1) * WIN], MSG[h][:, e, c * 128:(c + 1) * 128], SEL[h][:, e, :],
                                             start=e == 0, stop=e == EK - 1)
                    last.then_inc(win_full, 1)


def stray_stage(k, st):
    nc, sb, sem, A = k.nc, k.sb, k.sem, k.A
    EA = sb("stray_edge_attr", [128, EK, C], F32, st)
    GA = sb("stray_gathered", [128, EK, C], F32, st)
    MSG = sb("stray_message", [128, EK, C], F32, st)
    SEL = sb("stray_select", [128, EK, TR], F32, st)
    IDX = sb("stray_src", [128, EK], I32, st)
    dsti = sb("stray_dst_table", [128, NB, EK], I32, st)
    dst = sb("stray_dst", [128, NB, EK], F32, st)
    outside = sb("stray_outside", [128, NB, EK], F32, st)
    local = sb("stray_dst_in_tile", [128, EK], F32, st)
    dst_in, ea_in, g_in, idx_ready = (sem(n) for n in ("stray_dst_in", "stray_edge_attr_in", "stray_gathered_in", "stray_index_ready"))
    begun, sel_done, sums_full = (sem(n) for n in ("stray_gathers_begun", "stray_select_done", "stray_sums_full"))
    SUM = k.psum[0]

    def batches(eng, body):
        with eng.Fori(0, NB - 1) as b:
            body(b, b * EB)
        body(NB - 1, LAST)

    with nc.Block() as block:
        @block.sync
        def _(sp):
            there_are = sp.value_load(k.strays[0:1, 0:1], min_val=0, max_val=E)
            with sp.If(there_are > 0):
                sp.dma_start(dsti[:, 0:NB - 1, :], A["dst"][0:(NB - 1) * EB].rearrange("(b p k) -> p b k", p=128, k=EK)).then_inc(dst_in, 16)
                sp.dma_start(dsti[:, NB - 1, :], A["dst"][LAST:E].rearrange("(p k) -> p k", k=EK)).then_inc(dst_in, 16)

                def load(b, lo):
                    sp.wait_ge(idx_ready, b + 1)
                    sp.dma_start(EA[:, :, :], A["edge_attr_256"][bass.ds(lo, EB), :].rearrange("(p k) c -> p k c", k=EK)).then_inc(ea_in, 16)

                batches(sp, load)

        @block.gpsimd
        def _(pool):
            there_are = pool.value_load(k.strays[0:1, 0:1], min_val=0, max_val=E)
            with pool.If(there_are > 0):
                def gather(b, lo):
                    pool.wait_ge(idx_ready, b + 1)
                    pool.sem_inc(begun, 1)
                    for e in range(EK):
                        pool.indirect_dma_start(
                            out=GA[:, e, :], out_offset=None, in_=k.xn_d[:, :],
                            in_offset=bass.IndirectOffsetOnAxis(ap=IDX[:, e:e + 1], axis=0)).then_inc(g_in, 16)

                batches(pool, gather)

        @block.vector
        def _(dve):
            there_are = dve.value_load(k.strays[0:1, 0:1], min_val=0, max_val=E)
            with dve.If(there_are > 0):
                dve.wait_ge(dst_in, 32)
                dve.tensor_copy(dst[:, :, :], dsti[:, :, :])
                dve.tensor_scalar(outside[:, :, :], k.dstl[:, :, :], 0.0, None, ALU.is_lt)
                dve.tensor_scalar(k.dstl[:, :, :], k.dstl[:, :, :], float(WIN - 1), None, ALU.is_gt)
                dve.drain()
                dve.tensor_tensor(outside[:, :, :], outside[:, :, :], k.dstl[:, :, :], ALU.add)
                dve.tensor_scalar(dst[:, :, :], dst[:, :, :], 1.0, None, ALU.add)
                dve.drain()
                dve.tensor_tensor(dst[:, :, :], dst[:, :, :], outside[:, :, :], ALU.mult)
                dve.drain()
                dve.tensor_scalar(dst[:, :, :], dst[:, :, :], 1.0, None, ALU.subtract)
                dve.drain()

                def batch(b, lo):
                    dve.tensor_copy(IDX[:, :], k.src[:, bass.ds(b, 1), :].rearrange("p a k -> p (a k)")).then_inc(idx_ready, 1)
                    dve.tensor_copy(local[:, :], dst[:, bass.ds(b, 1), :].rearrange("p a k -> p (a k)"))
                    dve.wait_ge(ea_in, b * 16 + 16)
                    dve.wait_ge(g_in, b * (16 * EK) + 16 * EK)
                    dve.tensor_tensor(MSG[:, :, :], GA[:, :, :], EA[:, :, :], ALU.add)
                    dve.drain()
                    dve.tensor_scalar(MSG[:, :, :], MSG[:, :, :], 0.0, None, ALU.max)
                    dve.drain()
                    with dve.Fori(0, NT) as t:
                        for e in range(EK):
                            last = dve.tensor_scalar(SEL[:, e, :], k.iota[:, 0:TR], local[:, e:e + 1], None, ALU.is_equal)
                        last.then_inc(sel_done, 1)
                        dve.drain()
                        dve.tensor_scalar(local[:, :], local[:, :], float(TR), None, ALU.subtract)
                        dve.wait_ge(sums_full, b * NT + t + 1)
                        w = k.UT[:, :, bass.ds(t * TR, TR)]
                        dve.tensor_tensor(w, w, SUM[:, 0:CB * TR].rearrange("p (b n) -> p b n", b=CB), ALU.add)
                        dve.drain()

                batches(dve, batch)

        @block.tensor
        def _(pe):
            there_are = pe.value_load(k.strays[0:1, 0:1], min_val=0, max_val=E)
            with pe.If(there_are > 0):
                def batch(b, lo):
                    with pe.Fori(0, NT) as t:
                        pe.wait_ge(sel_done, b * NT + t + 1)
                        for c in range(CB):
                            for e in range(EK):
                                last = pe.matmul(SUM[:, c * TR:(c + 1) * TR], MSG[:, e, c * 128:(c + 1) * 128], SEL[:, e, :],
                                                 start=e == 0, stop=e == EK - 1)
                        last.then_inc(sums_full, 1)

                batches(pe, batch)


def gnn_mlp_stage(k, st):
    nc, sb, sem, A = k.nc, k.sb, k.sem, k.A
    W1 = sb("w1_gnn", [128, CB, HID], F32, st)
    W2 = sb("w2_gnn", [128, FB, C], F32, st)
    cols = sb("hidden_columns", [128, 3, FB], F32, st)
    outs = sb("out_columns", [128, 6, CB], F32, st)
    HT = sb("hiddenT", [128, FB, N], F32, st)
    ACTV = [sb(f"activated{h}", [128, FB, CH], F32, st) for h in range(2)]
    hst = sb("hidden_stats", [128, FB, NC, 6], F32, st)
    ost = sb("out_stats", [128, CB, NC, 6], F32, st)
    hmv = sb("hidden_mv", [128, FB, 2], F32, st)
    omv = sb("out_mv", [128, CB, 2], F32, st)
    sc = sb("hidden_scale", [128, 2, FB], F32, st)
    tmp = sb("graph_terms", [128, 8, CB], F32, st)
    gs = sb("graph_sums", [128, 6], F32, st)
    fill = sb("empty_row", [128, TT // 128, ROW], F32, st)
    w_in, col_in = sem("gnn_weights_in"), sem("gnn_columns_in")
    h_full, h_used = sem("hidden_full"), sem("hidden_copied")
    std_in, std_out, sc_done = sem("bn_var_ready"), sem("bn_std_ready"), sem("bn_scale_ready")
    a_done, o_full, o_used = sem("activated_done"), sem("out_full"), sem("out_copied")
    gsum_in, gsum_out, empty, empty_out = sem("graph_sum_in"), sem("graph_sum_out"), sem("empty_row_ready"), sem("empty_rows_out")
    HP = [k.psum[0:2], k.psum[2:4]]
    OP = k.psum[4:6]
    GP = k.psum[6]

    with nc.Block() as block:
        @block.sync
        def _(sp):
            sp.dma_start(W1[:, :, :], A["L0_gnn_W1"].rearrange("(b p) n -> p b n", p=128)).then_inc(w_in, 16)
            sp.dma_start(W2[:, :, :], A["L0_gnn_W2"].rearrange("(b p) n -> p b n", p=128)).then_inc(w_in, 16)
            with nc.allow_non_contiguous_dma("one word a partition"):
                for i, name in enumerate(("L0_gnn_b1", "L0_gnn_bn_gamma", "L0_gnn_bn_beta")):
                    sp.dma_start(cols[:, i, :], A[name].rearrange("(b p) -> p b", p=128)).then_inc(col_in, 16)
                for i, name in enumerate(("L0_gnn_b2", "L0_gnn_ln_w", "L0_gnn_ln_b", "L0_gnn_gn_w", "L0_gnn_gn_b", "L0_gnn_gn_ms")):
                    sp.dma_start(outs[:, i, :], A[name].rearrange("(b p) -> p b", p=128)).then_inc(col_in, 16)
            sp.wait_ge(empty, 3)
            for t in range(TT // 128):
                sp.dma_start(k.disp_d.rearrange("(i t p) c -> p t i c", p=128, t=TT // 128)[:, t, :, :],
                             fill[:, t, :].unsqueeze(1).to_broadcast([128, FT + 1, ROW])).then_inc(empty_out, 16)
            sp.dma_start(k.acc_d[N:N + TT, :].rearrange("(t p) c -> p t c", p=128), fill[:, :, 0:C]).then_inc(empty_out, 16)
            sp.wait_ge(empty_out, 16 * (TT // 128 + 1))

        @block.gpsimd
        def _(pool):
            pool.memset(fill[:, :, 0:ROW - 1], 0.0).then_inc(empty, 1)
            pool.iota(fill[:, :, ROW - 1].bitcast(I32), [[128, TT // 128]], base=N, channel_multiplier=1).then_inc(empty, 1)
            pool.drain().then_inc(empty, 1)

        @block.tensor
        def _(pe):
            pe.wait_ge(w_in, 32)

            def up(c, h):
                pe.wait_ge(h_used, c + 1)
                for f in range(FB):
                    for b in range(CB):
                        last = pe.matmul(HP[h][f // 2][:, (f % 2) * CH:(f % 2 + 1) * CH], W1[:, b, f * 128:(f + 1) * 128],
                                         k.UT[:, b, bass.ds(c * CH, CH)], start=b == 0, stop=b == CB - 1)
                last.then_inc(h_full, 1)

            pairs(pe, NC, up)

            def down(c, h):
                pe.wait_ge(a_done, c + 1)
                pe.wait_ge(o_used, c + 1)
                for q in range(CB):
                    for f in range(FB):
                        last = pe.matmul(OP[h][:, q * CH:(q + 1) * CH], W2[:, f, q * 128:(q + 1) * 128], ACTV[h][:, f, :],
                                         start=f == 0, stop=f == FB - 1)
                last.then_inc(o_full, 1)

            pairs(pe, NC, down)
            for n, w in ((0, 2), (1, 2)):
                pe.wait_ge(gsum_in, n + 1)
                pe.matmul(GP[:, n * 2:n * 2 + w], k.ones[:, :], tmp[:, n, 0:w], start=True, stop=True).then_inc(gsum_out, 1)

        @block.scalar
        def _(act):
            act.wait_ge(col_in, 16 * 9)

            def copy_out(c, h):
                act.wait_ge(h_full, c + 1)
                for f in range(FB):
                    last = act.activation(HT[:, f, bass.ds(c * CH, CH)], HP[h][f // 2][:, (f % 2) * CH:(f % 2 + 1) * CH],
                                          ACT.Identity, bias=cols[:, 0, f:f + 1])
                last.then_inc(h_used, 1)

            act.sem_inc(h_used, 2)
            pairs(act, NC, copy_out)
            act.wait_ge(std_in, 1)
            act.activation(sc[:, 0, :], hmv[:, :, 1], ACT.Sqrt, bias=k.eps[:, :]).then_inc(std_out, 1)
            act.wait_ge(sc_done, 1)

            def activate(c, h):
                if not first_two(c):
                    act.wait_ge(o_full, c - 1)
                else:
                    act.wait_ge(h_used, 2)
                for f in range(FB):
                    last = act.activation(ACTV[h][:, f, :], HT[:, f, bass.ds(c * CH, CH)], ACT.Relu,
                                          scale=sc[:, 0, f:f + 1], bias=sc[:, 1, f:f + 1])
                last.then_inc(a_done, 1)

            activate(0, 0)
            activate(1, 1)
            with act.Fori(1, NC // 2) as i:
                activate(i * 2, 0)
                activate(i * 2 + 1, 1)
            activate(NC - 1, 0)
            act.wait_ge(std_in, 2)
            act.activation(tmp[:, 2, 0:1], tmp[:, 2, 0:1], ACT.Sqrt, bias=k.eps[:, :]).then_inc(std_out, 1)
            act.wait_ge(std_in, 3)
            act.activation(tmp[:, 6, :], tmp[:, 6, :], ACT.Sqrt, bias=k.eps[:, :]).then_inc(std_out, 1)

        @block.vector
        def _(dve):
            def seen(c, h):
                dve.wait_ge(h_used, c + 3)
                for f in range(FB):
                    dve.bn_stats(hst[:, f, bass.ds(c, 1), :].rearrange("p a s -> p (a s)"), HT[:, f, bass.ds(c * CH, CH)])

            pairs(dve, NC, seen)
            dve.drain()
            for f in range(FB):
                dve.bn_aggr(hmv[:, f, :], hst[:, f, :, :])
            dve.drain()
            dve.sem_inc(std_in, 1)
            dve.wait_ge(std_out, 1)
            dve.reciprocal(sc[:, 0, :], sc[:, 0, :])
            dve.drain()
            dve.wait_ge(col_in, 16 * 9)
            dve.tensor_tensor(sc[:, 0, :], sc[:, 0, :], cols[:, 1, :], ALU.mult)
            dve.drain()
            dve.tensor_tensor(sc[:, 1, :], hmv[:, :, 0], sc[:, 0, :], ALU.mult)
            dve.drain()
            dve.tensor_tensor(sc[:, 1, :], cols[:, 2, :], sc[:, 1, :], ALU.subtract).then_inc(sc_done, 1)
            dve.sem_inc(o_used, 2)

            def copy_out(c, h):
                dve.wait_ge(o_full, c + 1)
                for q in range(CB):
                    dve.bn_stats(ost[:, q, bass.ds(c, 1), :].rearrange("p a s -> p (a s)"), OP[h][:, q * CH:(q + 1) * CH])
                for q in range(CB):
                    last = dve.tensor_scalar(k.UT[:, q, bass.ds(c * CH, CH)], OP[h][:, q * CH:(q + 1) * CH],
                                             outs[:, 0, q:q + 1], None, ALU.add)
                last.then_inc(o_used, 1)

            pairs(dve, NC, copy_out)
            dve.drain()
            for q in range(CB):
                dve.bn_aggr(omv[:, q, :], ost[:, q, :, :])
            dve.drain()

            b2, ln_w, ln_b, gn_w, gn_b, gn_ms = (outs[:, i, :] for i in range(6))
            mean, var = omv[:, :, 0], omv[:, :, 1]
            tt, ts = dve.tensor_tensor, dve.tensor_scalar
            tt(mean, mean, b2, ALU.add)
            dve.drain()
            dve.tensor_reduce(tmp[:, 0, 0:1], mean, AX.X, ALU.add)
            dve.memset(tmp[:, 0, 1:2], 0.0)
            dve.memset(tmp[:, 1, 1:2], 0.0)
            dve.drain()
            dve.sem_inc(gsum_in, 1)
            dve.wait_ge(gsum_out, 1)
            ts(gs[:, 0:1], GP[:, 0:1], 1.0 / C, None, ALU.mult)
            dve.drain()
            ts(tmp[:, 3, :], mean, gs[:, 0:1], None, ALU.subtract)
            dve.drain()
            tt(tmp[:, 3, :], tmp[:, 3, :], tmp[:, 3, :], ALU.mult)
            dve.drain()
            tt(tmp[:, 3, :], tmp[:, 3, :], var, ALU.add)
            dve.drain()
            dve.tensor_reduce(tmp[:, 1, 0:1], tmp[:, 3, :], AX.X, ALU.add)
            dve.drain()
            dve.sem_inc(gsum_in, 1)
            dve.wait_ge(gsum_out, 2)
            ts(tmp[:, 2, 0:1], GP[:, 2:3], 1.0 / C, None, ALU.mult)
            dve.drain()
            dve.sem_inc(std_in, 1)
            dve.wait_ge(std_out, 2)
            dve.reciprocal(gs[:, 1:2], tmp[:, 2, 0:1])
            dve.drain()
            ts(tmp[:, 3, :], ln_w, gs[:, 1:2], None, ALU.mult)
            dve.drain()
            ts(tmp[:, 4, :], tmp[:, 3, :], gs[:, 0:1], None, ALU.mult)
            tt(tmp[:, 5, :], tmp[:, 3, :], mean, ALU.mult)
            dve.drain()
            tt(tmp[:, 4, :], ln_b, tmp[:, 4, :], ALU.subtract)
            dve.drain()
            tt(tmp[:, 5, :], tmp[:, 5, :], tmp[:, 4, :], ALU.add)
            dve.drain()
            tt(tmp[:, 7, :], tmp[:, 5, :], gn_ms, ALU.mult)
            tt(tmp[:, 6, :], tmp[:, 3, :], tmp[:, 3, :], ALU.mult)
            dve.drain()
            tt(tmp[:, 5, :], tmp[:, 5, :], tmp[:, 7, :], ALU.subtract)
            tt(tmp[:, 6, :], tmp[:, 6, :], var, ALU.mult)
            dve.drain()
            tt(tmp[:, 5, :], tmp[:, 5, :], tmp[:, 5, :], ALU.mult)
            dve.drain()
            tt(tmp[:, 6, :], tmp[:, 6, :], tmp[:, 5, :], ALU.add)
            tt(tmp[:, 4, :], tmp[:, 4, :], tmp[:, 7, :], ALU.subtract)
            dve.drain()
            dve.sem_inc(std_in, 1)
            dve.wait_ge(std_out, 3)
            dve.reciprocal(tmp[:, 6, :], tmp[:, 6, :])
            dve.drain()
            tt(tmp[:, 6, :], tmp[:, 6, :], gn_w, ALU.mult)
            dve.drain()
            tt(k.gsc[:, :], tmp[:, 3, :], tmp[:, 6, :], ALU.mult)
            tt(k.gbi[:, :], tmp[:, 4, :], tmp[:, 6, :], ALU.mult)
            dve.drain()
            tt(k.gbi[:, :], k.gbi[:, :], gn_b, ALU.add)


def residual_stage(k, st):
    nc, sb, sem = k.nc, k.sb, k.sem
    G = 5
    NG = NT // G
    two = range(2)
    Z = [sb(f"activatedT{h}", [128, G, CB, TR], F32, st) for h in two]
    R = [sb(f"residual_in{h}", [TR, G, C], F32, st) for h in two]
    XN = [sb(f"tokens{h}", [TR, G, C], F32, st) for h in two]
    XT = [sb(f"tokensT{h}", [128, G, CB, TR], F32, st) for h in two]
    stats = sb("ln2_stats", [TR, G, 6], F32, st)
    mv = sb("ln2_mv", [TR, G, 2], F32, st)
    std = sb("ln2_std", [TR, G], F32, st)
    r_in = [sem(f"residual_rows_in{h}") for h in two]
    x1_out, tok_out = [sem(f"x1_out{h}") for h in two], [sem(f"token_rows_out{h}") for h in two]
    z_done, zt_full, x1_done, std_in, std_out, xn_done = (sem(n) for n in (
        "activatedT_done", "activated_rows_full", "x1_done", "ln2_var_ready", "ln2_std_ready", "tokens_done"))
    xt_full, xt_free, lg_full, lg_done = (sem(n) for n in (
        "tokensT_full", "tokensT_free", "logits_full", "logits_done"))
    ZP, XP, LP = k.psum[0:3], k.psum[3:5], k.psum[5]
    zp = lambda g: ZP[g // 2][0:TR, (g % 2) * C:(g % 2 + 1) * C]

    with nc.Block() as block:
        @block.sync
        def _(sp):
            def move(n, h):
                rows = bass.ds(n * (G * TR), G * TR)
                if not first_two(n):
                    sp.wait_ge(x1_out[h], moved(n, h))
                    sp.wait_ge(tok_out[h], moved(n, h))
                move_rows(sp, R[h][:, :, :], k.r_d[rows, :].rearrange("(g p) c -> p g c", g=G), r_in[h])

            pairs(sp, NG, move)

        @block.gpsimd
        def _(pool):
            def store(n, h):
                rows = bass.ds(n * (G * TR), G * TR)
                pool.wait_ge(x1_done, n + 1)
                pool.sem_inc(k.pool_turn, 1)
                move_rows(pool, k.acc_d[rows, :].rearrange("(g p) c -> p g c", g=G), R[h][:, :, :], x1_out[h])
                pool.wait_ge(xn_done, n + 1)
                pool.sem_inc(k.pool_turn, 1)
                move_rows(pool, k.tok_d[rows, 0:C].rearrange("(g p) c -> p g c", g=G), XN[h][:, :, :], tok_out[h])

            pairs(pool, NG, store)
            for h in two:
                pool.wait_ge(x1_out[h], MOVED * (NG // 2))
                pool.wait_ge(tok_out[h], MOVED * (NG // 2))

        @block.scalar
        def _(act):
            def activate(n, h):
                for g in range(G):
                    for b in range(CB):
                        last = act.activation(Z[h][:, g, b, :], k.UT[:, b, bass.ds(n * (G * TR) + g * TR, TR)], ACT.Relu,
                                              scale=k.gsc[:, b:b + 1], bias=k.gbi[:, b:b + 1])
                last.then_inc(z_done, 1)

            def logits(n):
                act.wait_ge(lg_full, n + 1)
                act.activation(k.LG[:, bass.ds(n * G, G), :], LP[0:TR, 0:G * NX].rearrange("p (g e) -> p g e", g=G),
                               ACT.Copy).then_inc(lg_done, 1)

            def rest(n, h, more):
                act.wait_ge(std_in, n + 1)
                act.activation(std[:, :], mv[:, :, 1], ACT.Sqrt, bias=k.eps[0:TR, :]).then_inc(std_out, 1)
                if more:
                    act.wait_ge(zt_full, n + 1)
                    activate(n + 2, h)
                for g in range(G):
                    act.wait_ge(xt_full, n * G + g + 1)
                    act.activation(XT[h][:, g, :, :], XP[g % 2][:, 0:CB * TR].rearrange("p (b n) -> p b n", b=CB),
                                   ACT.Copy).then_inc(xt_free, 1)
                if not the_first(n):
                    logits(n - 1)

            act.sem_inc(xt_free, 2)
            act.sem_inc(lg_done, 1)
            activate(0, 0)
            activate(1, 1)
            rest(0, 0, True)
            rest(1, 1, True)
            with act.Fori(1, NG // 2 - 1) as i:
                for h in two:
                    rest(i * 2 + h, h, True)
            rest(NG - 2, 0, False)
            rest(NG - 1, 1, False)
            logits(NG - 1)

        @block.tensor
        def _(pe):
            def turn(n, h):
                pe.wait_ge(z_done, n + 1)
                if not the_first(n):
                    pe.wait_ge(x1_done, n)
                for g in range(G):
                    for b in range(CB):
                        last = pe.transpose(zp(g)[:, b * 128:(b + 1) * 128], Z[h][:, g, b, :], k.ident[:, :])
                last.then_inc(zt_full, 1)

            def logits(n, h):
                pe.wait_ge(xt_free, n * G + G + 2)
                pe.wait_ge(lg_done, n + 1)
                for g in range(G):
                    for b in range(CB):
                        last = pe.matmul(LP[0:TR, g * NX:(g + 1) * NX], XT[h][:, g, b, :], k.rwT[:, b, :], start=b == 0, stop=b == CB - 1)
                last.then_inc(lg_full, 1)

            def rest(n, h, more):
                if more:
                    turn(n + 1, 1 - h)
                if not the_first(n):
                    logits(n - 1, 1 - h)
                pe.wait_ge(xn_done, n + 1)
                for g in range(G):
                    m = n * G + g
                    pe.wait_ge(xt_free, m + 1 if g else m + 2)
                    for b in range(CB):
                        last = pe.transpose(XP[g % 2][:, b * TR:(b + 1) * TR], XN[h][:, g, b * 128:(b + 1) * 128], k.ident[0:TR, 0:TR])
                    last.then_inc(xt_full, 1)

            turn(0, 0)
            rest(0, 0, True)
            rest(1, 1, True)
            with pe.Fori(1, NG // 2 - 1) as i:
                for h in two:
                    rest(i * 2 + h, h, True)
            rest(NG - 2, 0, True)
            rest(NG - 1, 1, False)
            logits(NG - 1, 1)

        @block.vector
        def _(dve):
            def norm(n, h):
                dve.wait_ge(r_in[h], moved(n, h) + MOVED)
                dve.wait_ge(zt_full, n + 1)
                for z in range(0, G, 2):
                    w = min(2, G - z)
                    last = dve.tensor_tensor(R[h][:, z:z + w, :], R[h][:, z:z + w, :],
                                             ZP[z // 2][0:TR, 0:w * C].rearrange("p (g c) -> p g c", g=w), ALU.add)
                last.then_inc(x1_done, 1)
                dve.drain()
                for g in range(G):
                    dve.bn_stats(stats[:, g, :], R[h][:, g, :])
                dve.drain()
                for g in range(G):
                    dve.bn_aggr(mv[:, g, :], stats[:, g, :])
                dve.drain()
                dve.sem_inc(std_in, 1)
                dve.wait_ge(std_out, n + 1)
                dve.reciprocal(std[:, :], std[:, :])
                dve.drain()
                if not first_two(n):
                    dve.wait_ge(tok_out[h], moved(n, h))
                    dve.wait_ge(xt_full, n * G - G)
                for g in range(G):
                    last = dve.tensor_scalar(XN[h][:, g, :], R[h][:, g, :], mv[:, g, 0:1], std[:, g:g + 1], ALU.subtract, ALU.mult)
                last.then_inc(xn_done, 1)

            pairs(dve, NG, norm)


def moe_stage(k, st):
    W = k.sb("expert_weights", [128, NX, 2, WL], F16, st)
    te = k.sb("tile_expert", [1, FT + 1], I32, st)
    tef = k.sb("tile_expert_rows", [128, FT + 1], F32, st)
    used = k.sb("tiles_used", [1, 1], I32, st)
    with ExitStack() as low:
        dispatch_stage(k, low, W, te, tef, used)
    for lo, hi in ((0, USUAL), (USUAL, FT)):
        with ExitStack() as low:
            expert_stage(k, low, W, te, tef, used, lo, hi)
    out_stage(k)


def dispatch_stage(k, st, W, te, tef, used):
    nc, sb, sem, A = k.nc, k.sb, k.sem, k.A
    two = range(2)
    RAW = [sb(f"raw_weights{m}", [128, HB * C], F32, st) for m in range(3)]
    ST = 5
    NS = NT // ST
    XS = [sb(f"rows_to_send{h}", [TR, ST, ROW], F32, st) for h in two]
    IX = [sb(f"send_index{h}", [TR, ST, 2], I32, st) for h in two]
    sh = [TR, NT, NX]
    T = lambda name, shape=sh, dt=F32: sb(name, shape, dt, st)
    prob, w1, w2, oh1, oh2, oh = (T(n) for n in ("probs", "rank1", "rank2", "choice1", "choice2", "chosen"))
    m1, m2, f1, f2, den = (T(n, [TR, NT]) for n in ("top1", "top2", "first1", "first2", "gate_sum"))
    run = [T(f"running{h}", [128, NT, NX]) for h in two]
    cnt = [T(f"expert_ends{h}", [128, NX]) for h in two]
    tiles, tilesi, base = T("expert_tiles", [128, NX]), T("expert_tiles_i", [128, NX], I32), T("expert_base", [128, NX])
    tri, iof, iot, back = T("earlier_partition", [TR, TR]), T("iota_tiles", [128, FT + 1]), T("tile_past", [128, FT + 1, NX]), T("back_rank", [TR, NX])
    pos, extra, ids = T("row_of_pair", [TR, NT, 2], I32), T("row_extras", [TR, NT, 4]), T("token_ids", [TR, NT], I32)
    posf = T("row_of_pair_f", [TR, NT, 2])
    raw_in = [sem(f"raw_weights_in{m}") for m in range(3)]
    wt_full, wt_hi, wt_lo = sem("weightsT_full"), sem("weights_high"), sem("weights_low")
    ready, shifted, exped, routed, ranks, extra_done, extra_out = (sem(n) for n in (
        "route_consts", "logits_shifted", "exp_done", "routed", "ranks_full", "extras_done", "extras_out"))
    xs_in, sent = [sem(f"rows_to_send_in{h}") for h in two], [sem(f"rows_sent{h}") for h in two]
    ix_done, blank = sem("send_index_done"), sem("blank_weights")
    PB = [k.psum[0:3], k.psum[3:6]]
    part = lambda e, p, lo, n: W[:, bass.ds(e, 1), p:p + 1, lo:lo + n].rearrange("q a b n -> q (a b n)")
    pair = lambda e, p, lo, n: part(e, p, lo, 2 * n).rearrange("q (k h) -> q k h", k=2)

    def pieces(m, e, p):
        if m < 2:
            at = m * CB * HM
            rest = lambda b: b[2][:, :].rearrange("p (k h) -> p k h", k=2)
            return [(lambda b: b[0][:, :], part(e, p, at, 512), SW), (lambda b: b[1][:, :], part(e, p, at + HM, 512), SW),
                    (lambda b: rest(b)[:, :, 0:128], pair(e, p, at, HM)[:, :, 512:HM], SW),
                    (lambda b: rest(b)[:, :, C - TAIL:C], pair(e, p, TAILS, 128)[:, :, m * TAIL3:m * TAIL3 + TAIL], SW)]
        n = T3.stop
        return [(lambda b: b[0][:, :], part(e, p, W2S, 512), SW), (lambda b: b[1][:, :], part(e, p, W2S + 512, 512), SW),
                (lambda b: b[2][:, 0:C], part(e, p, W2S + 4 * C, C), SW),
                (lambda b: b[2][0:n, C:2 * C], part(e, p, W2S + 5 * C, C)[0:n, :], k.hmask[0:n, :])]

    def experts(eng, body):
        with eng.Fori(0, NX // 2) as i:
            for h in two:
                for m in range(3):
                    body(i * 2 + h, m, i * 6 + (3 * h + m), (3 * h + m) % 2)

    with nc.Block() as block:
        @block.sync
        def _(sp):
            def load(e, m, n, s):
                sp.wait_ge(wt_full, n + 1)
                if m < 2:
                    w = A[("L0_ffn_w1", "L0_ffn_w3")[m]][bass.ds(e, 1), :, :].rearrange("a h c -> (a h) c")
                    dst = RAW[m][:, :].rearrange("p (j c) -> p j c", c=C)
                    sp.dma_start(dst[:, 0:HB - 1, :], w[0:128 * (HB - 1), :].rearrange("(j p) c -> p j c", p=128)).then_inc(raw_in[m], 16)
                    sp.dma_start(dst[:, HB - 1, :], w[H - 128:H, :]).then_inc(raw_in[m], 16)
                else:
                    sp.dma_start(RAW[m][:, 0:CB * H].rearrange("p (b h) -> p b h", b=CB),
                                 A["L0_ffn_w2"][bass.ds(e, 1), :, :].rearrange("a (b p) h -> p (a b) h", p=128)).then_inc(raw_in[m], 16)

            experts(sp, load)

        @block.gpsimd
        def _(pool):
            pool.memset(tri[:, :], 1.0).then_inc(ready, 1)
            pool.iota(back[:, :], [[-1, NX]], base=NX, channel_multiplier=0, allow_small_or_imprecise_dtypes=True).then_inc(ready, 1)
            pool.iota(iof[:, :], [[1, FT + 1]], base=0, channel_multiplier=0, allow_small_or_imprecise_dtypes=True).then_inc(ready, 1)
            pool.iota(ids[:, :], [[TR, NT]], base=0, channel_multiplier=1).then_inc(ready, 1)
            pool.drain()
            pool.affine_select(out=tri[:, :], in_=tri[:, :], compare_op=ALU.is_gt, fill=0.0, base=0,
                               pattern=[[1, TR]], channel_multiplier=-1).then_inc(ready, 1)
            pool.memset(W[:, :, :, TAILS:W2S], 0.0).then_inc(blank, 1)
            pool.memset(W[:, :, :, WL - C:WL], 0.0).then_inc(blank, 1)
            pool.wait_ge(routed, 1)

            def send(n, h):
                if not first_two(n):
                    pool.wait_ge(sent[h], (n - h) * (16 * ST))
                    pool.sem_inc(k.pool_turn, 1)
                pool.tensor_copy(IX[h][:, :, :], pos[:, bass.ds(n * ST, ST), :]).then_inc(ix_done, 1)
                pool.wait_ge(ix_done, n + 1)
                pool.wait_ge(xs_in[h], moved(n, h) + MOVED)
                pool.sem_inc(k.pool_turn, 1)
                for t in range(ST):
                    for c in two:
                        pool.indirect_dma_start(out=k.disp_d[:, :], out_offset=bass.IndirectOffsetOnAxis(ap=IX[h][:, t, c:c + 1], axis=0),
                                                in_=XS[h][:, t, :], in_offset=None).then_inc(sent[h], 16)

            pairs(pool, NS, send)
            for h in two:
                pool.wait_ge(sent[h], 32 * ST * (NS // 2))

        @block.scalar
        def _(act):
            act.wait_ge(shifted, 1)
            act.activation(prob[:, :, :], prob[:, :, :], ACT.Exp).then_inc(exped, 1)
            with nc.allow_non_contiguous_dma("four words of each token"):
                act.wait_ge(extra_done, 1)
                act.dma_start(k.tok_d.rearrange("(t p) c -> p t c", p=TR)[:, :, C:ROW], extra[:, :, :]).then_inc(extra_out, 16)
            act.wait_ge(extra_out, 16)

            act.wait_ge(blank, 2)

            def high(e, m, n, s):
                act.wait_ge(wt_full, n + 4)
                for cols, to, scale in pieces(m, e, 0):
                    last = act.activation(to, cols(PB[s]), ACT.Copy, scale=scale)
                last.then_inc(wt_hi, 1)

            def load(n, h):
                if not first_two(n):
                    act.wait_ge(sent[h], (n - h) * (16 * ST))
                move_rows(act, XS[h][:, :, :], k.tok_d[bass.ds(n * (ST * TR), ST * TR), :].rearrange("(t p) c -> p t c", t=ST), xs_in[h])

            load(0, 0)
            load(1, 1)
            with act.Fori(0, NX // 2) as i:
                for h in two:
                    for m in range(3):
                        high(i * 2 + h, m, i * 6 + (3 * h + m), (3 * h + m) % 2)
                    load(i * 2 + h + 2, h)

        @block.tensor
        def _(pe):
            pe.wait_ge(ready, 5)
            pe.wait_ge(ranks, 1)
            flat = oh[:, :, :].rearrange("p t e -> p (t e)")
            pe.matmul(k.psum[6][0:TR, 0:NT * NX], tri[:, :], flat, start=True, stop=True)
            pe.matmul(k.psum[7][:, 0:NT * NX], k.ones[0:TR, :], flat, start=True, stop=True).then_inc(ranks, 1)

            def turn(e, m, n, s):
                pe.wait_ge(raw_in[m], e * (32 if m < 2 else 16) + (32 if m < 2 else 16))
                pe.wait_ge(wt_lo, n + 1)
                if m < 2:
                    src = RAW[m][:, :].rearrange("p (j c) -> p j c", c=C)
                    for b in range(CB):
                        for j in range(4):
                            pe.transpose(PB[s][b][:, j * 128:(j + 1) * 128], src[:, j, b * 128:(b + 1) * 128], k.ident[:, :])
                        for j in range(4, HB):
                            last = pe.transpose(PB[s][2][:, b * C + (j - 4) * 128:b * C + (j - 3) * 128], src[:, j, b * 128:(b + 1) * 128], k.ident[:, :])
                else:
                    for j in range(HB):
                        h0, n = (128 * j, 128) if j < HB - 1 else (HM - TAIL3, TAIL3 + TAIL)
                        for b in range(CB):
                            last = pe.transpose(PB[s][j // 2][0:n, (j % 2) * C + b * 128:(j % 2) * C + (b + 1) * 128],
                                                RAW[m][:, b * H + h0:b * H + h0 + n], k.ident[:, :])
                last.then_inc(wt_full, 1)

            experts(pe, turn)

        @block.vector
        def _(dve):
            tt, ts, red, drain = dve.tensor_tensor, dve.tensor_scalar, dve.tensor_reduce, dve.drain
            wide = lambda a: a.unsqueeze(2).to_broadcast(sh)
            dve.sem_inc(wt_full, 3)
            dve.sem_inc(wt_lo, 2)
            red(m1[:, :], k.LG[:, :, :], AX.X, ALU.max)
            drain()
            tt(prob[:, :, :], k.LG[:, :, :], wide(m1[:, :]), ALU.subtract).then_inc(shifted, 1)
            dve.wait_ge(exped, 1)
            red(den[:, :], prob[:, :, :], AX.X, ALU.add)
            drain()
            dve.reciprocal(den[:, :], den[:, :])
            drain()
            tt(prob[:, :, :], prob[:, :, :], wide(den[:, :]), ALU.mult)
            drain()
            dve.wait_ge(ready, 5)
            for m, f, w, o in ((m1, f1, w1, oh1), (m2, f2, w2, oh2)):
                red(m[:, :], prob[:, :, :], AX.X, ALU.max)
                drain()
                tt(w[:, :, :], prob[:, :, :], wide(m[:, :]), ALU.is_equal)
                drain()
                tt(w[:, :, :], w[:, :, :], back[:, :].unsqueeze(1).to_broadcast(sh), ALU.mult)
                drain()
                red(f[:, :], w[:, :, :], AX.X, ALU.max)
                drain()
                tt(o[:, :, :], w[:, :, :], wide(f[:, :]), ALU.is_equal)
                drain()
                if o is oh1:
                    dve.scalar_tensor_tensor(prob[:, :, :], o[:, :, :], -2.0, prob[:, :, :], ALU.mult, ALU.add)
                    drain()
            tt(oh[:, :, :], oh1[:, :, :], oh2[:, :, :], ALU.add)
            drain()
            dve.sem_inc(ranks, 1)
            tt(den[:, :], m1[:, :], m2[:, :], ALU.add)
            drain()
            ts(den[:, :], den[:, :], 1e-9, None, ALU.add)
            drain()
            dve.reciprocal(den[:, :], den[:, :])
            drain()
            for i, m in enumerate((m1, m2)):
                dve.scalar_tensor_tensor(extra[:, :, i], m[:, :], 1.0 / (SG * SW), den[:, :], ALU.mult, ALU.mult)
            ts(extra[:, :, 2], f1[:, :], -1.0, float(NX), ALU.mult, ALU.add)
            dve.tensor_copy(extra[:, :, 3].bitcast(I32), ids[:, :])
            drain()
            dve.sem_inc(extra_done, 1)
            dve.wait_ge(ranks, 2)
            tot = k.psum[7][:, 0:NT * NX].rearrange("p (t e) -> p t e", e=NX)
            dve.tensor_copy(run[0][:, :, :], tot)
            drain()
            step, cur = 1, 0
            while step < NT:
                a, b = run[cur], run[1 - cur]
                tt(b[:, step:NT, :], a[:, step:NT, :], a[:, 0:NT - step, :], ALU.add)
                dve.tensor_copy(b[:, 0:step, :], a[:, 0:step, :])
                drain()
                step, cur = step * 2, 1 - cur
            acc = run[cur]
            ts(tiles[:, :], acc[:, NT - 1, :], TT - 1.0, None, ALU.add)
            drain()
            dve.tensor_copy(tilesi[:, :], tiles[:, :])
            drain()
            ts(tilesi[:, :], tilesi[:, :], TT.bit_length() - 1, None, ALU.arith_shift_right)
            drain()
            dve.tensor_copy(tiles[:, :], tilesi[:, :])
            drain()
            dve.tensor_copy(cnt[0][:, :], tiles[:, :])
            drain()
            step, c = 1, 0
            while step < NX:
                a, b = cnt[c], cnt[1 - c]
                tt(b[:, step:NX], a[:, step:NX], a[:, 0:NX - step], ALU.add)
                dve.tensor_copy(b[:, 0:step], a[:, 0:step])
                drain()
                step, c = step * 2, 1 - c
            ends = cnt[c]
            tt(base[:, :], ends[:, :], tiles[:, :], ALU.subtract)
            drain()
            ts(base[:, :], base[:, :], float(TT), None, ALU.mult)
            tt(acc[:, :, :], acc[:, :, :], tot, ALU.subtract)
            drain()
            tt(acc[0:TR, :, :], acc[0:TR, :, :], k.psum[6][0:TR, 0:NT * NX].rearrange("p (t e) -> p t e", e=NX), ALU.add)
            drain()
            tt(acc[0:TR, :, :], acc[0:TR, :, :], base[0:TR, :].unsqueeze(1).to_broadcast(sh), ALU.add)
            drain()
            for i, (o, w) in enumerate(((oh1, w1), (oh2, w2))):
                tt(w[:, :, :], o[:, :, :], acc[0:TR, :, :], ALU.mult)
                drain()
                red(posf[:, :, i], w[:, :, :], AX.X, ALU.add)
            drain()
            dve.tensor_copy(pos[:, :, :], posf[:, :, :])
            tt(iot[:, :, :], iof[:, :].unsqueeze(2).to_broadcast([128, FT + 1, NX]),
               ends[:, :].unsqueeze(1).to_broadcast([128, FT + 1, NX]), ALU.is_ge)
            drain()
            red(tef[:, :], iot[:, :, :], AX.X, ALU.add)
            drain()
            ts(tef[:, :], tef[:, :], float(NX - 1), None, ALU.min)
            drain()
            dve.tensor_copy(te[:, :], tef[0:1, :])
            dve.tensor_copy(used[:, :], ends[0:1, NX - 1:NX])
            drain()
            dve.sem_inc(routed, 1)

            def low(e, m, n, s):
                dve.wait_ge(wt_hi, n + 1)
                for (cols, to, scale), (_, hi, _) in zip(pieces(m, e, 1), pieces(m, e, 0)):
                    last = dve.scalar_tensor_tensor(to, cols(PB[s]), scale, hi, ALU.mult, ALU.subtract)
                last.then_inc(wt_lo, 1)

            experts(dve, low)
            drain()
            tail = W[:, :, 0, WL - C:WL]
            dve.tensor_copy(tail[0:TAIL], tail[T3])


def expert_stage(k, st, W, te, tef, used, lo, hi):
    nc, NTILES = k.nc, hi - lo
    sb = lambda name, *a: k.sb(f"{name}_{lo}", *a)
    sem = lambda name: k.sem(f"{name}_{lo}")
    two = range(2)
    TB = TT // 128
    JB = 512 // TT
    SN = HB // JB
    XG = [sb(f"rows{h}", [128, TB, ROW], F32, st) for h in two]
    X16 = [sb(f"rowsT_parts{h}", [128, 2, CB, TT], F16, st) for h in two]
    SIL = [sb(f"silu{s}", [128, 512], F32, st) for s in two]
    GF = [sb(f"gated{s}", [128, 512], F32, st) for s in two]
    G16 = [sb(f"gated_parts{h}", [128, 2, HB * TT], F16, st) for h in two]
    YS = [sb(f"expert_out{h}", [128, TB, C], F32, st) for h in two]
    IDS = [sb(f"token_index{h}", [128, TB], I32, st) for h in two]
    gate = sb("row_gates", [128, NTILES + 1, TB], F32, st)
    token = sb("row_tokens", [128, NTILES + 1, TB], I32, st)
    gd = sb("gate_terms", [128, 2, TB], F32, st)
    xg_in = [sem(f"rows_in{h}") for h in two]
    xt_full, x_hi, x_done = sem("rowsT_full"), sem("rowsT_high"), sem("rowsT_done")
    h_full, silu_done, g_done, g_hi, g_lo = (sem(n) for n in ("hidden_step_full", "silu_done", "gated_done", "gated_high", "gated_low"))
    y_full, y_done, y_index, added, landed, pe_turn, act_turn, g_blank = (sem(n) for n in (
        "expert_psum_full", "expert_out_done", "expert_index_done", "rows_added", "rows_landed", "pe_turn", "act_turn", "gated_blank"))
    H1, H3, XP, YP = k.psum[0:2], k.psum[2:4], k.psum[4], k.psum[5:7]

    def reached(eng):
        if lo == 0:
            return ExitStack()
        return eng.If(eng.value_load(used[0:1, 0:1], min_val=0, max_val=FT) > lo)

    def tiles(eng, body):
        body(0, 0, False, False)
        body(1, 1, False, True)
        if NTILES // 2 > 1:
            with eng.Fori(1, NTILES // 2) as i:
                for h in two:
                    body(i * 2 + h, h, True, True)
        for i in range(NTILES // 2 * 2, NTILES):
            body(i, i % 2, True, True)

    def w(e, part, lo, n):
        return W[:, bass.ds(e, 1), part:part + 1, lo:lo + n].rearrange("q a b n -> q (a b n)")

    def halves(s):
        if s < SN - 1:
            return [(slice(0, 128), slice(0, 512), False)]
        return [(slice(0, 128), slice(0, 512 - TT), False), (T3, slice(512 - TT, 512), True)]

    with nc.Block() as block:
        @block.sync
        def _(sp):
            with reached(sp):
                def load(i, h):
                    sp.wait_ge(x_done, i + 1)
                    sp.dma_start(XG[h][:, :, :], k.disp_d[bass.ds(i * TT + lo * TT, TT), :].rearrange("(t p) c -> p t c", t=TB)).then_inc(xg_in[h], 16)

                pairs(sp, NTILES + 1, load)
                sp.wait_ge(added, 16 * TB * NTILES)

        @block.gpsimd
        def _(pool):
            with reached(pool):
                for h in two:
                    pool.memset(G16[h][:, :, (HB - 1) * TT:HB * TT], 0.0).then_inc(g_blank, 1)

                def add(i, h):
                    pool.wait_ge(y_done, i + 3)
                    pool.wait_ge(y_index, i + 1)
                    if not the_first(i):
                        pool.wait_ge(added, i * (16 * TB))
                    pool.sem_inc(landed, 1)
                    for t in range(TB):
                        pool.indirect_dma_start(out=k.acc_d[:, :], out_offset=bass.IndirectOffsetOnAxis(ap=IDS[h][:, t:t + 1], axis=0),
                                                in_=YS[h][:, t, :], in_offset=None, compute_op=ALU.add).then_inc(added, 16)

                pairs(pool, NTILES, add)

        @block.tensor
        def _(pe):
            with reached(pe):
                def turn(i, h):
                    pe.wait_ge(xg_in[h], (i - h) * 8 + 16)
                    pe.wait_ge(x_done, i + 2)
                    for b in range(CB):
                        for t in range(TB):
                            last = pe.transpose(XP[:, b * TT + t * 128:b * TT + (t + 1) * 128], XG[h][:, t, b * 128:(b + 1) * 128], k.ident[:, :])
                    last.then_inc(xt_full, 1)

                def hidden(i, h, s, e):
                    r = (SN * h + s) % 2
                    pe.wait_ge(x_done, i + 3)
                    pe.wait_ge(g_done, i * SN + s + 1)
                    pe.sem_inc(pe_turn, 1)
                    for m, bank in ((0, H1[r]), (1, H3[r])):
                        for jj in range(JB):
                            if s == SN - 1 and jj == JB - 1:
                                if m == 1:
                                    continue
                                at, step = TAILS, 128
                            else:
                                at, step = m * CB * HM + (JB * s + jj) * 128, HM
                            n = 0
                            for b in range(CB):
                                for wp, xp in ((0, 0), (0, 1), (1, 0)):
                                    last = pe.matmul(bank[:, jj * TT:(jj + 1) * TT], w(e, wp, at + b * step, 128),
                                                     X16[h][:, xp, b, :], start=n == 0, stop=n == 3 * CB - 1)
                                    n += 1
                    last.then_inc(h_full, 1)

                def down(i, h, e):
                    pe.wait_ge(g_lo, (i + 1) * SN)
                    pe.wait_ge(y_done, i + 1)
                    for t in range(TB):
                        n = 0
                        for j in range(HB):
                            for gp, wp in ((0, 0), (0, 1), (1, 0))[0:3 if j < HB - 1 else 2]:
                                last = pe.matmul(YP[h][:, t * C:(t + 1) * C], G16[h][:, gp, j * TT + t * 128:j * TT + (t + 1) * 128],
                                                 w(e, wp, W2S + j * C, C), start=n == 0, stop=n == 3 * HB - 2)
                                n += 1
                    last.then_inc(y_full, 1)

                expert_of = lambda i: pe.value_load(te[0:1, bass.ds(i + lo, 1)], min_val=0, max_val=NX - 1)
                turn(0, 0)

                def tile(i, h, _, before):
                    e = expert_of(i)
                    eb = expert_of(i - 1) if before else None
                    for s in range(SN):
                        hidden(i, h, s, e)
                        if s == 0:
                            turn(i + 1, 1 - h)
                    if before:
                        down(i - 1, 1 - h, eb)

                tiles(pe, tile)
                down(NTILES - 1, (NTILES - 1) % 2, expert_of(NTILES - 1))

        @block.scalar
        def _(act):
            with reached(act):
                def rows_high(i, h):
                    act.wait_ge(xt_full, i + 1)
                    act.activation(X16[h][:, 0, :, :], XP[:, :].rearrange("p (b n) -> p b n", b=CB), ACT.Copy, scale=SX).then_inc(x_hi, 1)

                def step(i, h, s):
                    r = (SN * h + s) % 2
                    act.wait_ge(h_full, i * SN + s + 1)
                    for at, cols, tail in halves(s):
                        last = act.activation(SIL[r][at, cols], H1[r][0:TAIL if tail else 128, cols], ACT.Silu, scale=1.0 / (SX * SW))
                    last.then_inc(silu_done, 1)
                    act.wait_ge(g_done, i * SN + s + 3)
                    for at, cols, tail in halves(s):
                        last = act.activation(G16[h][at, 0, s * 512 + cols.start:s * 512 + cols.stop], GF[r][at, cols], ACT.Copy)
                    last.then_inc(g_hi, 1)

                def out(i, h):
                    act.wait_ge(y_full, i + 1)
                    act.wait_ge(landed, i + 1)
                    act.sem_inc(act_turn, 1)
                    for t in range(TB):
                        act.activation(YS[h][:, t, :], YP[h][:, t * C:(t + 1) * C], ACT.Copy,
                                       scale=gate[:, bass.ds(i, 1), t:t + 1].rearrange("p a t -> p (a t)"))
                    act.drain()
                    act.sem_inc(y_done, 1)

                rows_high(0, 0)
                act.wait_ge(g_blank, 2)

                def tile(i, h, before2, before):
                    for s in range(SN):
                        step(i, h, s)
                        if s == 0:
                            rows_high(i + 1, 1 - h)
                            if before2:
                                out(i - 2, h)

                tiles(act, tile)
                for i in (NTILES - 2, NTILES - 1):
                    out(i, i % 2)

        @block.vector
        def _(dve):
            with reached(dve):
                dve.sem_inc(x_done, 2)
                dve.sem_inc(g_done, 2)
                dve.sem_inc(y_done, 2)
                dve.sem_inc(landed, 1)

                def rows_low(i, h):
                    dve.wait_ge(x_hi, i + 1)
                    dve.wait_ge(xg_in[h], (i - h) * 8 + 16)
                    dve.scalar_tensor_tensor(X16[h][:, 1, :, :], XP[:, :].rearrange("p (b n) -> p b n", b=CB), SX,
                                             X16[h][:, 0, :, :], ALU.mult, ALU.subtract)
                    word = lambda n: XG[h][:, :, C + n]
                    flat = lambda a: a[:, bass.ds(i, 1), :].rearrange("p a t -> p (a t)")
                    dve.tensor_tensor(gd[:, 0, :], word(0), word(1), ALU.subtract)
                    dve.tensor_scalar(gd[:, 1, :], word(2), tef[:, bass.ds(i + lo, 1)], None, ALU.is_equal)
                    dve.tensor_copy(flat(token), word(3).bitcast(I32))
                    dve.drain()
                    dve.tensor_tensor(gd[:, 0, :], gd[:, 0, :], gd[:, 1, :], ALU.mult)
                    dve.drain()
                    dve.tensor_tensor(flat(gate), gd[:, 0, :], word(1), ALU.add)
                    dve.drain()
                    dve.sem_inc(x_done, 1)

                def step(i, h, s):
                    r = (SN * h + s) % 2
                    dve.wait_ge(silu_done, i * SN + s + 1)
                    for at, cols, tail in halves(s):
                        last = dve.scalar_tensor_tensor(GF[r][at, cols], (H1 if tail else H3)[r][at, cols], SG / (SX * SW), SIL[r][at, cols],
                                                        ALU.mult, ALU.mult)
                    last.then_inc(g_done, 1)
                    dve.wait_ge(g_hi, i * SN + s + 1)
                    for at, cols, tail in halves(s):
                        to = slice(s * 512 + cols.start, s * 512 + cols.stop)
                        low = G16[h][0:TAIL, 0, to] if tail else G16[h][at, 1, to]
                        last = dve.tensor_tensor(low, GF[r][at, cols], G16[h][at, 0, to], ALU.subtract)
                    last.then_inc(g_lo, 1)

                def index(i, h):
                    dve.wait_ge(landed, i + 1)
                    dve.tensor_copy(IDS[h][:, :], token[:, bass.ds(i, 1), :].rearrange("p a t -> p (a t)")).then_inc(y_index, 1)

                rows_low(0, 0)

                def tile(i, h, before2, before):
                    for s in range(SN):
                        step(i, h, s)
                        if s == 0:
                            rows_low(i + 1, 1 - h)
                            if before2:
                                index(i - 2, h)

                tiles(dve, tile)
                for i in (NTILES - 2, NTILES - 1):
                    index(i, i % 2)


def out_stage(k):
    out_done = k.sem("out_written")
    with k.nc.Block() as block:
        @block.sync
        def _(sp):
            flat = lambda a: a.rearrange("n c -> (n c)").rearrange("(a m) -> a m", a=128)
            sp.dma_start(flat(k.out), flat(k.acc_d[0:N, :])).then_inc(out_done, 16)
            sp.wait_ge(out_done, 16)


_INS = ['x', 'src', 'dst', 'edge_attr_256', 'L0_gnn_W1', 'L0_gnn_b1', 'L0_gnn_bn_gamma', 'L0_gnn_bn_beta', 'L0_gnn_W2',
        'L0_gnn_b2', 'L0_gnn_ln_w', 'L0_gnn_ln_b', 'L0_gnn_gn_w', 'L0_gnn_gn_b', 'L0_gnn_gn_ms', 'L0_mix_W_qkv',
        'L0_mix_b_qkv', 'L0_mix_W_out', 'L0_mix_b_out', 'L0_ffn_router_w', 'L0_ffn_w1', 'L0_ffn_w2', 'L0_ffn_w3']


def kernel(**inputs):
    import numpy as np
    import concourse.bacc as bacc
    from concourse.bass_utils import run_bass_kernel_spmd

    nc = bacc.Bacc("TRN2", target_bir_lowering=False, num_devices=1)
    arrays, aps = {}, {}
    for name in _INS:
        a = np.ascontiguousarray(inputs[name])
        arrays[f"in_{name}"] = a
        aps[name] = nc.dram_tensor(f"in_{name}", a.shape, mybir.dt.from_np(a.dtype), kind="ExternalInput").ap()
    out = nc.dram_tensor("out", (N, C), F32, kind="ExternalOutput").ap()
    build(nc, aps, out)
    r = run_bass_kernel_spmd(nc, [arrays], core_ids=[0])
    return r.results[0]["out"]
```
